# Optimizing a Trainium2 kernel written in Bass

```python
import numpy as np
import jax
import jax.numpy as jnp

def _softmax(x, axis=-1):
    return jax.nn.softmax(x, axis=axis)

def _gelu(x):
    return jax.nn.gelu(x, approximate=True)

def _silu(x):
    return jax.nn.silu(x)

def _sigmoid(x):
    return jax.nn.sigmoid(x)

def _layernorm(x, axis=-1, eps=1e-05):
    m = jnp.mean(x, axis=axis, keepdims=True)
    v = jnp.var(x, axis=axis, keepdims=True)
    return (x - m) / jnp.sqrt(v + eps)

def _scatter_add(tgt, idx, src, axis=0):
    return tgt.at[idx].add(src)

def _segment_sum(src, seg, n):
    return jax.ops.segment_sum(src, seg, n)
kernel_name = 'mk_decoder_preln_d1_seqx_r8_bef544'

def setup_inputs(seed: int=0):
    np.random.seed(seed)
    _w = jnp.asarray

    def _rec_inputs():
        import jax
        import jax.numpy as jnp
        _rk = jax.random.key(seed)
        x = -0.0005207 + 1.001 * jax.random.normal(jax.random.fold_in(_rk, 1), (4, 256, 128), jnp.float32)
        _lenS = 256 - jax.random.randint(jax.random.fold_in(_rk, 7), (4,), 0, max(1, 256 // 4) + 1, jnp.int32)
        _lenS2 = 256 - jax.random.randint(jax.random.fold_in(_rk, 8), (4,), 0, max(1, 256 // 4) + 1, jnp.int32)
        _ctx_1024P = jax.random.normal(jax.random.fold_in(_rk, 11), (4, 16, 128), jnp.float32)
        _ctx_1024c = jax.random.dirichlet(jax.random.fold_in(_rk, 511), 0.3 * jnp.ones((16,), jnp.float32), (4, 256))
        _ctx_1024t = jnp.einsum('bsk,bkd->bsd', _ctx_1024c, _ctx_1024P)
        _ctx_1024t = _ctx_1024t * jax.lax.rsqrt(jnp.mean(jnp.square(_ctx_1024t)) + 1e-12) * 0.953939
        ctx_1024 = -1.39393e-06 + 0.999914 * (_ctx_1024t + 0.3 * jax.random.normal(jax.random.fold_in(_rk, 611), (4, 256, 128), jnp.float32))
        return (x, ctx_1024)
    x, ctx_1024 = _rec_inputs()

    def _L0_attn_setup():
        import math
        import jax, jax.numpy as jnp
        import numpy as np
        B, S, H = (2, 256, 128)
        NH = 16
        HD = H // NH
        THETA = 10000.0

        def _rope_cache(seq_len, head_dim, theta):
            inv_freq = 1.0 / theta ** (jnp.arange(0, head_dim, 2, dtype=jnp.float32) / head_dim)
            pos = jnp.arange(seq_len, dtype=jnp.float32)
            freqs = jnp.outer(pos, inv_freq)
            emb = jnp.concatenate([freqs, freqs], -1)
            return (jnp.cos(emb), jnp.sin(emb))

        def _apply_rotary(x, cos, sin):
            d = x.shape[-1] // 2
            x1, x2 = (x[..., :d], x[..., d:])
            rotated = jnp.concatenate([-x2, x1], -1)
            return x * cos + rotated * sin
        key = jax.random.key(seed)
        ks = jax.random.split(key, 5)
        scale = 1.0 / math.sqrt(H)
        return {'x': jax.random.normal(ks[0], (B, S, H), jnp.float32), 'Wq': jax.random.normal(ks[1], (H, H), jnp.float32) * scale, 'Wk': jax.random.normal(ks[2], (H, H), jnp.float32) * scale, 'Wv': jax.random.normal(ks[3], (H, H), jnp.float32) * scale, 'Wo': jax.random.normal(ks[4], (H, H), jnp.float32) * scale}
    _L0_attn_all = _L0_attn_setup()
    _L0_attn_in = {k: v for k, v in _L0_attn_all.items() if k in ('Wq', 'Wk', 'Wv', 'Wo')}
    del _L0_attn_all

    def _L0_xattn_setup():
        import jax, jax.numpy as jnp
        import numpy as np
        DIM = 128
        HEADS = 16
        HEAD_DIM = DIM // HEADS
        SCALE = HEAD_DIM ** (-0.5)
        key = jax.random.key(seed)
        ks = jax.random.split(key, 6)
        B, Nq, Nkv = (2, 128, 256)
        s = DIM ** (-0.5)
        return {'x': jax.random.normal(ks[0], (B, Nq, DIM), jnp.float32), 'mem': jax.random.normal(ks[1], (B, Nkv, DIM), jnp.float32), 'W_kv': jax.random.normal(ks[2], (DIM, 2 * DIM), jnp.float32) * s, 'W_q': jax.random.normal(ks[3], (DIM, DIM), jnp.float32) * s, 'W_proj': jax.random.normal(ks[4], (DIM, DIM), jnp.float32) * s, 'b_proj': jax.random.normal(ks[5], (DIM,), jnp.float32) * 0.01}
    _L0_xattn_all = _L0_xattn_setup()
    _L0_xattn_in = {k: v for k, v in _L0_xattn_all.items() if k in ('W_kv', 'W_q', 'W_proj', 'b_proj')}
    del _L0_xattn_all

    def _L0_ffn_setup():
        import jax, jax.numpy as jnp
        import numpy as np
        B, T, H = (8, 256, 128)
        F = 512
        E = 8
        TOP_K = 2
        key = jax.random.key(seed)
        ks = jax.random.split(key, 6)
        s_h = 1.0 / np.sqrt(H)
        s_f = 1.0 / np.sqrt(F)
        return {'hidden_states': jax.random.normal(ks[0], (B, T, H), dtype=jnp.float32), 'gate_w': jax.random.uniform(ks[1], (H, E), minval=-s_h, maxval=s_h, dtype=jnp.float32), 'w1': jax.random.uniform(ks[2], (E, H, F), minval=-s_h, maxval=s_h, dtype=jnp.float32), 'b1': jax.random.uniform(ks[3], (E, F), minval=-s_h, maxval=s_h, dtype=jnp.float32), 'w2': jax.random.uniform(ks[4], (E, F, H), minval=-s_f, maxval=s_f, dtype=jnp.float32), 'b2': jax.random.uniform(ks[5], (E, H), minval=-s_f, maxval=s_f, dtype=jnp.float32)}
    _L0_ffn_all = _L0_ffn_setup()
    _L0_ffn_in = {k: v for k, v in _L0_ffn_all.items() if k in ('gate_w', 'w1', 'b1', 'w2', 'b2')}
    del _L0_ffn_all
    return {'x': x, 'ctx_1024': ctx_1024, 'L0_attn_Wq': _L0_attn_in['Wq'], 'L0_attn_Wk': _L0_attn_in['Wk'], 'L0_attn_Wv': _L0_attn_in['Wv'], 'L0_attn_Wo': _L0_attn_in['Wo'], 'L0_xattn_W_kv': _L0_xattn_in['W_kv'], 'L0_xattn_W_q': _L0_xattn_in['W_q'], 'L0_xattn_W_proj': _L0_xattn_in['W_proj'], 'L0_xattn_b_proj': _L0_xattn_in['b_proj'], 'L0_ffn_gate_w': _L0_ffn_in['gate_w'], 'L0_ffn_w1': _L0_ffn_in['w1'], 'L0_ffn_b1': _L0_ffn_in['b1'], 'L0_ffn_w2': _L0_ffn_in['w2'], 'L0_ffn_b2': _L0_ffn_in['b2']}

def reference(x, ctx_1024, L0_attn_Wq, L0_attn_Wk, L0_attn_Wv, L0_attn_Wo, L0_xattn_W_kv, L0_xattn_W_q, L0_xattn_W_proj, L0_xattn_b_proj, L0_ffn_gate_w, L0_ffn_w1, L0_ffn_b1, L0_ffn_w2, L0_ffn_b2):
    import jax
    import jax.numpy as jnp

    def _L0_attn_ref(x, Wq, Wk, Wv, Wo):
        import math
        import jax, jax.numpy as jnp
        import numpy as np
        B, S, H = (2, 256, 128)
        NH = 16
        HD = H // NH
        THETA = 10000.0

        def _rope_cache(seq_len, head_dim, theta):
            inv_freq = 1.0 / theta ** (jnp.arange(0, head_dim, 2, dtype=jnp.float32) / head_dim)
            pos = jnp.arange(seq_len, dtype=jnp.float32)
            freqs = jnp.outer(pos, inv_freq)
            emb = jnp.concatenate([freqs, freqs], -1)
            return (jnp.cos(emb), jnp.sin(emb))

        def _apply_rotary(x, cos, sin):
            d = x.shape[-1] // 2
            x1, x2 = (x[..., :d], x[..., d:])
            rotated = jnp.concatenate([-x2, x1], -1)
            return x * cos + rotated * sin
        b, s, h = x.shape
        q = (x @ Wq.T).reshape(b, s, NH, HD).transpose(0, 2, 1, 3)
        k = (x @ Wk.T).reshape(b, s, NH, HD).transpose(0, 2, 1, 3)
        v = (x @ Wv.T).reshape(b, s, NH, HD).transpose(0, 2, 1, 3)
        cos, sin = _rope_cache(s, HD, THETA)
        q = _apply_rotary(q, cos, sin)
        k = _apply_rotary(k, cos, sin)
        scale = 1.0 / math.sqrt(HD)
        attn = jnp.einsum('bhqd,bhkd->bhqk', q, k) * scale
        causal = jnp.triu(jnp.ones((s, s), dtype=bool), k=1)
        attn = jnp.where(causal, -jnp.inf, attn)
        attn = jax.nn.softmax(attn, axis=-1)
        out = jnp.einsum('bhqk,bhkd->bhqd', attn, v)
        out = out.transpose(0, 2, 1, 3).reshape(b, s, h)
        return out @ Wo.T

    def _L0_xattn_ref(x, mem, W_kv, W_q, W_proj, b_proj):
        import jax, jax.numpy as jnp
        import numpy as np
        DIM = 128
        HEADS = 16
        HEAD_DIM = DIM // HEADS
        SCALE = HEAD_DIM ** (-0.5)
        B, Nkv, C = mem.shape
        Nq = x.shape[1]
        kv = (mem @ W_kv).reshape(B, Nkv, 2, HEADS, HEAD_DIM)
        k = kv[:, :, 0].transpose(0, 2, 1, 3)
        v = kv[:, :, 1].transpose(0, 2, 1, 3)
        q = (x @ W_q).reshape(B, Nq, HEADS, HEAD_DIM).transpose(0, 2, 1, 3)
        attn = jnp.einsum('bhqd,bhkd->bhqk', q, k) * SCALE
        attn = jax.nn.softmax(attn, axis=-1)
        out = jnp.einsum('bhqk,bhkd->bhqd', attn, v)
        out = out.transpose(0, 2, 1, 3).reshape(B, Nq, C)
        return out @ W_proj + b_proj

    def _L0_ffn_ref(hidden_states, gate_w, w1, b1, w2, b2):
        import jax, jax.numpy as jnp
        import numpy as np
        B, T, H = (8, 256, 128)
        F = 512
        E = 8
        TOP_K = 2
        b, t, h = hidden_states.shape
        seq_rep = hidden_states.mean(axis=1)
        router_logits = seq_rep @ gate_w
        probs = jax.nn.softmax(router_logits.astype(jnp.float32), axis=-1)
        top_w, top_i = jax.lax.top_k(probs, TOP_K)
        top_w = top_w / top_w.sum(axis=-1, keepdims=True)
        top_w = top_w.astype(hidden_states.dtype)
        combine = jnp.zeros((b, E), dtype=hidden_states.dtype)
        combine = combine.at[jnp.arange(b)[:, None], top_i].set(top_w)
        out = jnp.zeros_like(hidden_states)
        for e in range(E):
            hmid = jax.nn.gelu(jnp.einsum('bth,hf->btf', hidden_states, w1[e]) + b1[e], approximate=False)
            y = jnp.einsum('btf,fh->bth', hmid, w2[e]) + b2[e]
            out = out + combine[:, e][:, None, None] * y
        return out
    x = x + _L0_attn_ref(_layernorm(x, axis=-1), L0_attn_Wq, L0_attn_Wk, L0_attn_Wv, L0_attn_Wo)
    x = x + _L0_xattn_ref(_layernorm(x, axis=-1), ctx_1024, L0_xattn_W_kv, L0_xattn_W_q, L0_xattn_W_proj, L0_xattn_b_proj)
    x = x + _L0_ffn_ref(_layernorm(x, axis=-1), L0_ffn_gate_w, L0_ffn_w1, L0_ffn_b1, L0_ffn_w2, L0_ffn_b2)
    return x

_drawn_inputs = setup_inputs


def setup_inputs(seed=0):
    import zlib

    import numpy as np

    out = dict(_drawn_inputs(seed))
    spreads = {}
    factors = {'L0_xattn_b_proj': 5.532, 'L0_ffn_b1': 4.914, 'L0_ffn_b2': 3.775}
    for name, (base, spread) in spreads.items():
        noise = np.random.default_rng([zlib.crc32(name.encode()), seed]).standard_normal(out[name].shape)
        drawn = base * np.exp(spread * noise) if base else spread * noise
        out[name] = jnp.asarray(drawn.astype(out[name].dtype))
    for name, factor in factors.items():
        out[name] = (out[name] * factor).astype(out[name].dtype)
    return out
```

```python
from contextlib import ExitStack

import concourse.bass as bass
from concourse import mybir

ALU = mybir.AluOpType
ACT = mybir.ActivationFunctionType
AX_X = mybir.AxisListType.X
F32 = mybir.dt.float32
BF16 = mybir.dt.bfloat16
U32 = mybir.dt.uint32

NB, S, D = 4, 256, 128
P = 128
NT = S // P
NH, HD = 16, 8
NG, GH = 4, 4
NE, TOPK, FF = 8, 2, 512
NC = FF // P
NPART = 3
ROWS = 96
MAXROW = 96
VW = 32
SCALE = float(HD) ** -0.5
EPS = 1e-5
MASKED = -2.0 ** 100
LAG = 6
NJOB = 2 * NB
GRP_UNITS = (3, 4)


def plan():
    before, after_a, after_b = {}, {}, {}

    def put(where, n, *step):
        where.setdefault(n, []).append(step)

    start = [("ln_stats", 0, 0), ("ln_apply", 0, 0), ("ln_turn", 0, 0), ("ln_stats", 0, 1), ("constants", 0, 0),
             ("ln_apply", 0, 1), ("init_stack", 0, 0), ("qk_self", 0, 0), ("ln_turn", 0, 1), ("stack_write", 0, 0),
             ("stack_read", 0, 0), ("init_v", 0, 0), ("v_self", 0, 0), ("qk_self", 0, 1), ("init_stack", 0, 1),
             ("stack_write", 0, 1), ("stack_read", 0, 1), ("init_v", 0, 1)]
    for b in (2, 3):
        n = 4 * b - 8
        put(after_b, n, "ln_stats", 0, b)
        put(after_a, n + 1, "ln_apply", 0, b)
        put(after_b, n + 1, "ln_turn", 0, b)
        put(after_b, n + 2, "qk_self", 0, b)
        put(after_b, n + 3, "init_stack", 0, b)
        put(after_b, n + 4, "stack_write", 0, b)
        put(after_b, n + 5, "stack_read", 0, b)
        put(after_b, n + 6, "init_v", 0, b)
    for b in range(1, NB):
        put(after_b, 4 * b, "v_self", 0, b)
    for j in range(NJOB):
        s, b = divmod(j, NB)
        n = 4 * j
        put(after_a, n + 4, "max_rows", s, b)
        put(after_a, n + 11, "o_turn", s, b)
        put(after_b, n + 11, "o_back", s, b)
        put(after_a, n + 12, "o_proj", s, b)
        put(after_a, n + 12, "ln_stats", s + 1, b)
        put(after_b, n + 12, "ln_apply", s + 1, b)
        put(after_a, n + 13, "ln_turn", s + 1, b)
        if s == 0:
            put(after_b, n + 9, "ctx_turn", 1, b)
            put(after_a, n + 10, "k_cross", 1, b)
            put(after_b, n + 12, "stack_write_k", 1, b)
            put(after_b, n + 12, "v_cross", 1, b)
            put(after_a, n + 13, "stack_read_k", 1, b)
            put(after_b, n + 13, "q_cross", 1, b)
            put(after_b, n + 13, "stack_write", 1, b)
            put(after_b, n + 14, "stack_read", 1, b)
        else:
            put(after_b, n + 13, "route", 2, b)
    ffn = [("moe_up", 0), ("moe_up", 1), ("moe_down", 0)]
    for n in range(2, 2 * NB):
        ffn += [("moe_up", n), ("moe_down", n - 1)]
        if n % 2 == 0:
            ffn.append(("moe_out", n - 1))
    ffn += [("moe_down", 2 * NB - 1), ("moe_out", 2 * NB - 1)]
    for n, k in ((38, 3), (39, 2), (40, 3), (41, 3)):
        for f in ffn[:k]:
            put(after_b, n, f[0], f[1] % 2, f[1] // 2)
        del ffn[:k]

    order = list(start)
    for n in range(NJOB * NG + 12):
        halves = [[], []]
        for kind, m in (("scores_max", n), ("scores_exp", n - LAG)):
            if 0 <= m < NJOB * NG:
                s, b = divmod(m // NG, NB)
                for u in range(GRP_UNITS[s]):
                    halves[u // 2].append((u, (kind, s, b, m % NG, u)))
        for half, extra in zip(range(2), (after_a, after_b)):
            order += [step for _, step in sorted(halves[half])]
            m = n - LAG - 1
            if 0 <= m < NJOB * NG:
                order.append(("values", *divmod(m // NG, NB), m % NG, half))
            order += extra.get(n, [])
    order += [(f[0], f[1] % 2, f[1] // 2) for f in ffn]

    uses = {"ln_turn": 1, "qk_self": 2, "v_self": 1, "ctx_turn": 1, "k_cross": 1, "v_cross": 1, "q_cross": 1,
            "max_rows": 1, "o_turn": 2, "o_back": 1, "o_proj": 1, "route": 1, "moe_out": 1}
    count, total, steps = [0, 0], 0, []
    a_unit = b_unit = norms = 0
    for kind, s, b, *g in order:
        misc = []
        for _ in range(uses.get(kind, 0)):
            bank = total % 2
            count[bank] += 1
            misc.append((bank, count[bank]))
            total += 1
        st = dict(kind=kind, s=s, b=b, g=g[0] if g else 0, u=g[1] if g else 0, misc=misc, unit=0, norm=norms)
        if kind == "scores_max":
            st["unit"] = a_unit
            a_unit += 1
        if kind == "scores_exp":
            st["unit"] = b_unit
            b_unit += 1
        if kind == "ln_turn":
            norms += 1
        steps.append(st)
    return steps, a_unit, b_unit


def a_units_until(job):
    return sum(NG * GRP_UNITS[j // NB] for j in range(job + 1))


def b_units_until(group):
    return sum(GRP_UNITS[n // (NG * NB)] for n in range(group + 1))


def build(nc, x, ctx_in, w_self, w_cross, b_proj, rope, gate_w, w1, b1, w2, b2, out):
    steps, a_total, b_total = plan()
    use = {(st["kind"], st["s"], st["b"]): st["misc"] for st in steps if st["misc"]}

    scratch_q = nc.dram_tensor("scratch_q", [2, NB, NPART, P, S], BF16).ap()
    scratch_k = nc.dram_tensor("scratch_k", [2, NB, NPART, P, S], BF16).ap()

    with ExitStack() as ctx:
        def sb(name, shape, dt=F32):
            return ctx.enter_context(nc.sbuf_tensor(name, shape, dt))

        def sem(name):
            return ctx.enter_context(nc.semaphore(name))

        def sems(name, n=NB):
            return [sem(f"{name}{i}") for i in range(n)]

        res = sb("res", [P, NB, NT, D])
        ctx_tok = sb("ctx_tok", [P, NB, NT, D])
        wS = sb("wS", [P, 6, D])
        wC = sb("wC", [P, 4, D])
        gate_sb = sb("gate_sb", [P, NE])
        rope_sb = sb("rope_sb", [P, 2, S])
        bproj = sb("bproj", [P, D])
        b1rows = sb("b1rows", [NE * NC, P])
        b2rows = sb("b2rows", [NE, D])
        b1T = sb("b1T", [P, NC, NE])
        b2T = sb("b2T", [P, NE])
        ident = sb("ident", [P, P])
        ident16 = sb("ident16", [P, P], BF16)
        mask16 = sb("mask16", [P, GH, P], BF16)
        mask16T = sb("mask16T", [P, GH, P], BF16)
        ones = sb("ones", [P, P])
        iota8 = sb("iota8", [P, NE])
        neg_half = sb("neg_half", [P, NT])
        euler = sb("euler", [P, NE])
        stats = sb("stats", [P, NB, NT, 6])
        mv = sb("mv", [P, NB, NT, 2])
        rstd = sb("rstd", [P, NB, NT])
        xn = sb("xn", [P, NB, NT, D])
        xnT = sb("xnT", [P, NB, S])
        ctxT = sb("ctxT", [P, NB, S])
        rot = sb("rot", [P, 2, 2, 2, S])
        kc = sb("kc", [P, 2, S])
        parts = sb("parts", [P, NB, 2, NPART, S], BF16)
        stackQ = sb("stackQ", [MAXROW + 2, NB, NH, S], BF16)
        stackK = sb("stackK", [MAXROW + 2, NB, NH, S], BF16)
        V = sb("V", [P, NB, NT, NH, VW])
        negmax = sb("negmax", [P, NB, NT * NH])
        maxT = sb("maxT", [NT * NH, NB, 2, P], BF16)
        E = sb("E", [P, 3, GH, NT, S])
        oT = sb("oT", [P, 2, NG, S])
        rden = sb("rden", [P, 2, NT, NH])
        oN = sb("oN", [P, 2, NT, D])
        oNT = sb("oNT", [P, 2, S])
        biased = sb("biased", [P, NT, D])
        seqsum = sb("seqsum", [P, NB, 1])
        small = sb("small", [P, NB, 16, NE])
        top_i = sb("top_i", [P, NB, NE], U32)
        b1pick = sb("b1pick", [P, NB, TOPK, NC])
        b1tmp = sb("b1tmp", [P, NC, NE])
        b2pick = sb("b2pick", [P, NB, 1])
        NW = 3
        w1s = sb("w1s", [P, NW, FF])
        w2s = sb("w2s", [P, NW, NC, D])
        hid = sb("hid", [P, 2, NC, S])
        yT = sb("yT", [P, S])

        psA = ctx.enter_context(nc.psum_tensor("psA", [P, 2, 512], F32))
        psB = ctx.enter_context(nc.psum_tensor("psB", [P, 2, 512], F32))
        psV = ctx.enter_context(nc.psum_tensor("psV", [P, 2, 512], F32))
        psM = ctx.enter_context(nc.psum_tensor("psM", [P, 2, 512], F32))

        x_in, ctx_loaded = sems("x_in"), sem("ctx_loaded")
        wS_in, wC_in, rope_in = sem("wS_in"), sem("wC_in"), sem("rope_in")
        rows_in, gate_in, bproj_in = sem("rows_in"), sem("gate_in"), sem("bproj_in")
        ident_set, consts, stack_init, v_init = sem("ident_set"), sem("consts"), sems("stack_init"), sem("v_init")
        misc_full, misc_taken = sems("misc_full", 2), sems("misc_taken", 2)
        bias_turned = sem("bias_turned")
        var_ready, rstd_ready, xn_ready = sem("var_ready"), sem("rstd_ready"), sem("xn_ready")
        parts_self, parts_k, parts_q = sems("parts_self"), sems("parts_k"), sems("parts_q")
        kc_ready, kc_split = sem("kc_ready"), sem("kc_split")
        rope_split = sem("rope_split")
        scr_q, scr_k = sems("scr_q"), sems("scr_k")
        q_in, k_in, maxrow_in = sems("q_in"), sems("k_in"), sems("maxrow_in")
        a_full, a_taken = sem("a_full"), sem("a_taken")
        b_full, b_taken = sem("b_full"), sem("b_taken")
        v_full, v_taken = sem("v_full"), sem("v_taken")
        oN_ready = sem("oN_ready")
        shifted, probs_ready = sem("shifted"), sem("probs_ready")
        seqrep = sem("seqrep")
        chosen = sem("chosen")
        w1_in, w2_in, w2_scaled = sems("w1_in", NW), sems("w2_in", NW), sem("w2_scaled")
        up_full, gelu_done, down_done = sem("up_full"), sem("gelu_done"), sem("down_done")
        y_taken = sem("y_taken")
        stored = sem("stored")
        dve_own, pool_own, act_own = sem("dve_own"), sem("pool_own"), sem("act_own")

        block = ctx.enter_context(nc.Block())

        @block.sync
        def _(sp):
            for b in range(NB):
                sp.dma_start(res[:, b], x[b].rearrange("(t p) d -> p t d", p=P)).then_inc(x_in[b], 16)
                if b == 0:
                    sp.dma_start(wS[:, :, :], w_self).then_inc(wS_in, 16)
                    sp.dma_start(rope_sb[:, :, :], rope).then_inc(rope_in, 16)
            sp.dma_start(ctx_tok[:, :, :, :],
                         ctx_in.rearrange("b (t p) d -> p (b t) d", p=P)).then_inc(ctx_loaded, 16)
            sp.dma_start(wC[:, :, :], w_cross).then_inc(wC_in, 16)
            sp.dma_start(b1rows[:, :], b1.rearrange("e (c p) -> (e c) p", p=P)).then_inc(rows_in, 16)
            sp.dma_start(b2rows[:, :], b2).then_inc(rows_in, 16)
            sp.dma_start(gate_sb[:, :], gate_w).then_inc(gate_in, 16)
            sp.dma_start(bproj[:, :], b_proj.partition_broadcast(P)).then_inc(bproj_in, 16)

            def write_parts(s, b, which, scratch, done):
                sp.dma_start(scratch[s, b].rearrange("i p t -> p i t"),
                             parts[:, b, which]).then_inc(done, 16)

            def read_q(s, b):
                sp.wait_ge(scr_q[b], 16 * (s + 1))
                for i in range(NPART):
                    r = i * NPART * HD
                    src = scratch_q[s, b, i]
                    thrice = bass.AP(src.tensor, src.offset, [[0, NPART], [NH * S, HD], [1, NH * S]])
                    sp.dma_start(stackQ[r:r + NPART * HD, b], thrice).then_inc(q_in[b], 16)

            def read_k(s, b):
                sp.wait_ge(scr_k[b], 16 * (s + 1))
                for i in range(NPART):
                    r = i * NPART * HD
                    sp.dma_start(stackK[r:r + NPART * HD, b],
                                 scratch_k[s, b].rearrange("i (d h) t -> (i d) h t", h=NH)).then_inc(k_in[b], 16)

            expert = 0
            for st in steps:
                kind, s, b = st["kind"], st["s"], st["b"]
                if kind == "stack_write" and s == 0:
                    sp.wait_ge(parts_self[b], 1)
                    write_parts(s, b, 0, scratch_q, scr_q[b])
                    write_parts(s, b, 1, scratch_k, scr_k[b])
                if kind == "stack_read" and s == 0:
                    sp.wait_ge(stack_init[b], 2)
                    read_q(s, b)
                    read_k(s, b)
                if kind == "stack_write_k":
                    sp.wait_ge(parts_k[b], 1)
                    write_parts(s, b, 1, scratch_k, scr_k[b])
                if kind == "stack_read_k":
                    sp.wait_ge(b_full, b_units_until(NG * (b + 1) - 1))
                    read_k(s, b)
                if kind == "stack_write" and s == 1:
                    sp.wait_ge(parts_q[b], 1)
                    write_parts(s, b, 0, scratch_q, scr_q[b])
                if kind == "stack_read" and s == 1:
                    read_q(s, b)
                if kind == "max_rows":
                    sp.wait_ge(misc_taken[st["misc"][0][0]], st["misc"][0][1])
                    for i in range(2):
                        for t in range(NT):
                            sp.dma_start(stackQ[MAXROW + i:MAXROW + i + 1, b, :, t * P:(t + 1) * P],
                                         maxT[t * NH:(t + 1) * NH, b, i, :]).then_inc(maxrow_in[b], 16)
                if kind == "route":
                    sp.wait_ge(chosen, b + 1)
                    for k in range(TOPK):
                        n = b * TOPK + k
                        e = sp.value_load(top_i[0:1, b, k:k + 1], min_val=0, max_val=NE - 1)
                        if n >= NW:
                            sp.wait_ge(down_done, n - NW + 1)
                        sp.dma_start(w1s[:, n % NW, :],
                                     w1[bass.ds(e, 1)].rearrange("e p f -> p (e f)")).then_inc(w1_in[n % NW], 16)
                        sp.dma_start(w2s[:, n % NW, :, :],
                                     w2[bass.ds(e, 1)].rearrange("e (c p) d -> p (e c) d", p=P)).then_inc(w2_in[n % NW], 16)
                if kind == "moe_out":
                    sp.wait_ge(misc_taken[st["misc"][0][0]], st["misc"][0][1])
                    sp.dma_start(out[b].rearrange("(t p) d -> p t d", p=P), res[:, b]).then_inc(stored, 16)
            sp.wait_ge(stored, 16 * NB)

        @block.gpsimd
        def _(pool):
            own = [0]

            def then(ins):
                own[0] += 1
                ins.then_inc(pool_own, 1)
                pool.wait_ge(pool_own, own[0])

            def constants():
                pool.memset(ones[:, :], 1.0).then_inc(consts, 1)
                pool.memset(euler[:, :], 2.718281828459045).then_inc(consts, 1)
                pool.iota(iota8[:, :], pattern=[[1, NE]], base=0, channel_multiplier=0,
                          allow_small_or_imprecise_dtypes=True).then_inc(consts, 1)
                then(pool.memset(ident16[:, :], 0.0))
                pool.affine_select(out=ident16[:, :], in_=ident16[:, :], compare_op=ALU.not_equal, fill=1.0, base=0,
                                   pattern=[[-1, P]], channel_multiplier=1).then_inc(consts, 1)
                for m, sign in ((mask16, 1), (mask16T, -1)):
                    then(pool.memset(m[:, :, :], 0.0))
                    pool.affine_select(out=m[:, :, :], in_=m[:, :, :], compare_op=ALU.is_ge, fill=MASKED, base=0,
                                       pattern=[[0, GH], [-sign, P]], channel_multiplier=sign).then_inc(consts, 1)

            then(pool.memset(neg_half[:, :], -0.5))
            then(pool.memset(ident[:, :], 0.0))
            pool.affine_select(out=ident[:, :], in_=ident[:, :], compare_op=ALU.not_equal, fill=1.0, base=0,
                               pattern=[[-1, P]], channel_multiplier=1).then_inc(ident_set, 1)

            def init_v(b):
                then(pool.memset(V[:, b], 0.0))
                pool.memset(V[:, b, :, :, HD:HD + 1], 1.0).then_inc(v_init, 1)
                pool.wait_ge(v_init, b + 1)

            def init_stack(b):
                pool.memset(stackQ[0:ROWS, b].bitcast(F32), 0.0).then_inc(stack_init[b], 1)
                pool.memset(stackK[:, b].bitcast(F32), ONES16).then_inc(stack_init[b], 1)

            def rsqrt_var(n, b):
                pool.wait_ge(var_ready, n + 1)
                then(pool.tensor_scalar(rstd[:, b, :], mv[:, b, :, 1], EPS, None, ALU.add))
                pool.tensor_tensor(rstd[:, b, :], rstd[:, b, :], neg_half[:, :], ALU.pow).then_inc(rstd_ready, 1)
                pool.wait_ge(rstd_ready, n + 1)

            for st in steps:
                kind, s, b, misc, unit = st["kind"], st["s"], st["b"], st["misc"], st["unit"]
                if kind == "ln_stats":
                    rsqrt_var(st["norm"], b)
                if kind == "constants":
                    constants()
                if kind == "init_v":
                    init_v(b)
                if kind == "init_stack" and b > 0:
                    init_stack(b)
                if kind == "qk_self" and b >= 1:
                    for bank, k in misc:
                        pool.wait_ge(misc_taken[bank], k)
                    cs, sn = rot[:, b % 2, 0], rot[:, b % 2, 1]
                    then(pool.tensor_tensor(cs, cs, sn, ALU.add))
                    for i in range(NPART - 1):
                        then(pool.tensor_copy(parts[:, b, :, i], cs))
                        then(pool.tensor_tensor(cs, cs, parts[:, b, :, i], ALU.subtract))
                    pool.tensor_copy(parts[:, b, :, NPART - 1], cs).then_inc(parts_self[b], 1)
                if kind == "k_cross":
                    bank, k = misc[0]
                    pool.wait_ge(misc_taken[bank], k)
                    kk = kc[:, b % 2]
                    for i in range(NPART - 1):
                        then(pool.tensor_copy(parts[:, b, 1, i], kk))
                        then(pool.tensor_tensor(kk, kk, parts[:, b, 1, i], ALU.subtract))
                    pool.tensor_copy(parts[:, b, 1, NPART - 1], kk).then_inc(parts_k[b], 1)
                if kind == "route":
                    pool.wait_ge(shifted, b + 1)
                    pool.tensor_tensor(small[:, b, 1], euler[:, :], small[:, b, 0], ALU.pow).then_inc(probs_ready, 1)

        @block.vector
        def _(dve):
            own = [0]

            def then(ins):
                own[0] += 1
                ins.then_inc(dve_own, 1)
                dve.wait_ge(dve_own, own[0])

            def split(src, dst, ready):
                for i in range(NPART - 1):
                    then(dve.tensor_copy(dst[:, i] if len(dst.shape) == 3 else dst[:, :, i], src))
                    then(dve.tensor_tensor(src, src, dst[:, i] if len(dst.shape) == 3 else dst[:, :, i], ALU.subtract))
                i = NPART - 1
                dve.tensor_copy(dst[:, i] if len(dst.shape) == 3 else dst[:, :, i], src).then_inc(ready, 1)

            biases = False
            for st in steps:
                kind, s, b, g, misc, unit = st["kind"], st["s"], st["b"], st["g"], st["misc"], st["unit"]
                job = s * NB + b
                if kind == "ln_stats":
                    if s == 0:
                        dve.wait_ge(x_in[b], 16)
                    for t in range(NT):
                        last = dve.bn_stats(stats[:, b, t, :], res[:, b, t, :])
                        if t == NT - 1:
                            then(last)
                    for t in range(NT):
                        last = dve.bn_aggr(mv[:, b, t, :], stats[:, b, t, :])
                    last.then_inc(var_ready, 1)
                if kind == "ln_apply":
                    dve.wait_ge(rstd_ready, st["norm"] + 1)
                    for t in range(NT):
                        last = dve.tensor_scalar(xn[:, b, t, :], res[:, b, t, :], mv[:, b, t, 0:1], rstd[:, b, t:t + 1],
                                                 ALU.subtract, ALU.mult)
                    last.then_inc(xn_ready, 1)
                if kind == "init_stack" and b == 0:
                    dve.memset(stackQ[64:ROWS, 0].bitcast(F32), 0.0).then_inc(stack_init[0], 1)
                    dve.memset(stackK[64:MAXROW + 2, 0].bitcast(F32), ONES16).then_inc(stack_init[0], 1)
                if kind == "qk_self":
                    if b == 0:
                        dve.wait_ge(rope_in, 16)
                    if b == 3:
                        dve.wait_ge(parts_self[b - 2], 1)
                    for i, (bank, k) in enumerate(misc):
                        dve.wait_ge(misc_full[bank], k)
                        table = rope_sb[:, i:i + 1, :].to_broadcast([P, 2, S])
                        dve.tensor_tensor(rot[:, b % 2, i], psM[:, bank].rearrange("p (a t) -> p a t", a=2), table,
                                          ALU.mult).then_inc(misc_taken[bank], 1)
                    if b == 0:
                        for bank, k in misc:
                            dve.wait_ge(misc_taken[bank], k)
                        cs = rot[:, b % 2, 0]
                        then(dve.tensor_tensor(cs, cs, rot[:, b % 2, 1], ALU.add))
                        split(cs, parts[:, b], parts_self[b])
                if kind == "q_cross":
                    bank, k = misc[0]
                    dve.wait_ge(misc_full[bank], k)
                    qq, dst = rot[:, b % 2, 0, 0], parts[:, b, 0]
                    then(dve.tensor_copy(dst[:, 0], psM[:, bank, 0:S]))
                    dve.tensor_tensor(qq, psM[:, bank, 0:S], dst[:, 0], ALU.subtract).then_inc(misc_taken[bank], 1)
                    dve.wait_ge(misc_taken[bank], k)
                    then(dve.tensor_copy(dst[:, 1], qq))
                    dve.tensor_tensor(dst[:, 2], qq, dst[:, 1], ALU.subtract).then_inc(parts_q[b], 1)
                if kind == "scores_max":
                    u, bank = st["u"], unit % 2
                    dve.wait_ge(a_full, unit + 1)
                    if s == 0 and u == 0:
                        cols, nh = g * GH, GH
                    elif s == 0:
                        cols, nh = NH + g * GH + 2 * (u - 1), 2
                    else:
                        cols, nh = (u // 2) * NH + g * GH + 2 * (u % 2), 2
                    dve.tensor_reduce(negmax[:, b, cols:cols + nh], psA[:, bank].rearrange("p (h k) -> p h k", h=nh),
                                      AX_X, ALU.max, negate=True).then_inc(a_taken, 1)
                if kind == "max_rows":
                    bank, k = misc[0]
                    dve.wait_ge(misc_full[bank], k)
                    if s == 1:
                        dve.wait_ge(maxrow_in[b], 64)
                    m = psM[0:NT * NH, bank, 0:P]
                    then(dve.tensor_copy(maxT[:, b, 0, :], m))
                    dve.tensor_tensor(maxT[:, b, 1, :], m, maxT[:, b, 0, :], ALU.subtract).then_inc(misc_taken[bank], 1)
                if kind == "o_turn":
                    for t, (bank, k) in enumerate(misc):
                        dve.wait_ge(misc_full[bank], k)
                        o = psM[:, bank].rearrange("p (h c) -> p h c", c=VW)
                        then(dve.reciprocal(rden[:, job % 2, t, :], o[:, :, HD]))
                        r = rden[:, job % 2, t, :].rearrange("p (h o) -> p h o", o=1).to_broadcast([P, NH, HD])
                        dve.tensor_tensor(oN[:, job % 2, t, :].rearrange("p (h c) -> p h c", c=HD), o[:, :, 0:HD], r,
                                          ALU.mult).then_inc(misc_taken[bank], 1)
                if kind == "o_proj":
                    bank, k = misc[0]
                    dve.wait_ge(misc_full[bank], k)
                    y = psM[:, bank, 0:S].rearrange("p (t d) -> p t d", t=NT)
                    if s == 0:
                        dve.tensor_tensor(res[:, b], res[:, b], y, ALU.add).then_inc(misc_taken[bank], 1)
                    else:
                        if b == 0:
                            dve.wait_ge(bproj_in, 16)
                        dve.tensor_tensor(biased[:, :, :], y,
                                          bproj[:, :].rearrange("p (o d) -> p o d", o=1).to_broadcast([P, NT, D]),
                                          ALU.add).then_inc(misc_taken[bank], 1)
                        dve.wait_ge(misc_taken[bank], k)
                        then(dve.tensor_tensor(res[:, b], res[:, b], biased[:, :, :], ALU.add))
                    dve.wait_ge(misc_taken[bank], k)
                if kind == "route":
                    bank, k = misc[0]
                    if not biases:
                        biases = True
                    turned = use[("ln_turn", 2, b)][0]
                    dve.wait_ge(misc_taken[turned[0]], turned[1])
                    dve.tensor_scalar(xn[:, b, 0, :], ones[:, :], seqsum[:, b, 0:1], 1.0 / S, ALU.mult,
                                      ALU.mult).then_inc(seqrep, 1)
                    dve.wait_ge(misc_full[bank], k)
                    v = small[:, b]
                    dve.tensor_copy(v[:, 2], psM[:, bank, 0:NE]).then_inc(misc_taken[bank], 1)
                    dve.wait_ge(misc_taken[bank], k)
                    then(dve.tensor_reduce(v[:, 3, 0:1], v[:, 2], AX_X, ALU.max))
                    dve.tensor_scalar(v[:, 0], v[:, 2], v[:, 3, 0:1], None, ALU.subtract).then_inc(shifted, 1)
                    dve.wait_ge(probs_ready, b + 1)
                    then(dve.max(v[:, 4], v[:, 1]))
                    dve.max_index(top_i[:, b, :], v[:, 4], v[:, 1]).then_inc(chosen, 1)
                    then(dve.tensor_tensor(v[:, 5, 0:1], v[:, 4, 0:1], v[:, 4, 1:2], ALU.add))
                    then(dve.reciprocal(v[:, 5, 1:2], v[:, 5, 0:1]))
                    then(dve.tensor_scalar(v[:, 6, 0:TOPK], v[:, 4, 0:TOPK], v[:, 5, 1:2], None, ALU.mult))
                    dve.wait_ge(chosen, b + 1)
                    then(dve.tensor_copy(v[:, 7], top_i[:, b, :]))
                    for n in range(TOPK):
                        then(dve.tensor_scalar(v[:, 8 + n], iota8[:, :], v[:, 7, n:n + 1], None, ALU.is_equal))
                        hot = v[:, 8 + n:9 + n].to_broadcast([P, NC, NE])
                        then(dve.tensor_tensor(b1tmp[:, :, :], b1T[:, :, :], hot, ALU.mult))
                        then(dve.tensor_reduce(b1pick[:, b, n, :], b1tmp[:, :, :], AX_X, ALU.add))
                        then(dve.tensor_scalar(v[:, 10 + n], v[:, 8 + n], v[:, 6, n:n + 1], None, ALU.mult))
                    then(dve.tensor_tensor(v[:, 12], v[:, 10], v[:, 11], ALU.add))
                    then(dve.tensor_tensor(v[:, 13], v[:, 12], b2T[:, :], ALU.mult))
                    then(dve.tensor_reduce(b2pick[:, b, :], v[:, 13], AX_X, ALU.add))
                if kind == "moe_up":
                    n = b * TOPK + s
                    dve.wait_ge(w2_in[n % NW], 16 * (n // NW + 1))
                    dve.tensor_scalar(w2s[:, n % NW], w2s[:, n % NW], small[:, b, 6, s:s + 1], None,
                                      ALU.mult).then_inc(w2_scaled, 1)
                if kind == "moe_out":
                    bank, k = misc[0]
                    dve.wait_ge(down_done, TOPK * (b + 1))
                    dve.tensor_scalar(yT[:, :], psV[:, b % 2, 0:S], b2pick[:, b, 0:1], None, ALU.add).then_inc(y_taken, 1)
                    dve.wait_ge(misc_full[bank], k)
                    dve.tensor_tensor(res[:, b], res[:, b], psM[:, bank, 0:S].rearrange("p (t d) -> p t d", t=NT),
                                      ALU.add).then_inc(misc_taken[bank], 1)
                if kind == "v_self" and b == 0:
                    dve.wait_ge(bias_turned, 1)
                    dve.tensor_copy(b1T[:, :, :],
                                    psV[:, 0, 0:NE * NC].rearrange("p (e c) -> p c e", c=NC)).then_inc(v_taken, 1)
                    dve.tensor_copy(b2T[:, :], psV[:, 0, NE * NC:NE * NC + NE]).then_inc(v_taken, 1)

        @block.scalar
        def _(act):
            for st in steps:
                kind, s, b, g, misc, unit = st["kind"], st["s"], st["b"], st["g"], st["misc"], st["unit"]
                job = s * NB + b
                if kind == "ln_turn":
                    bank, k = misc[0]
                    act.wait_ge(misc_full[bank], k)
                    if s < 2:
                        act.activation(xnT[:, b, :], psM[:, bank, 0:S], ACT.Copy).then_inc(misc_taken[bank], 1)
                    else:
                        act.activation(xnT[:, b, :], psM[:, bank, 0:S], ACT.Copy,
                                       accum_out=seqsum[:, b, 0:1]).then_inc(misc_taken[bank], 1)
                if kind == "ctx_turn":
                    bank, k = misc[0]
                    act.wait_ge(misc_full[bank], k)
                    act.activation(ctxT[:, b, :], psM[:, bank, 0:S], ACT.Copy).then_inc(misc_taken[bank], 1)
                if kind in ("v_self", "v_cross"):
                    bank, k = misc[0]
                    act.wait_ge(misc_full[bank], k)
                    if kind == "v_self":
                        act.wait_ge(v_init, b + 1)
                    else:
                        act.wait_ge(v_full, NG * (b + 1))
                    act.activation(V[:, b, :, :, 0:HD],
                                   psM[:, bank, 0:S].rearrange("p (t h d) -> p t h d", t=NT, h=NH),
                                   ACT.Copy).then_inc(misc_taken[bank], 1)
                if kind == "k_cross":
                    bank, k = misc[0]
                    act.wait_ge(misc_full[bank], k)
                    if b >= 2:
                        act.wait_ge(parts_k[b - 2], 1)
                    act.activation(kc[:, b % 2], psM[:, bank, 0:S], ACT.Copy).then_inc(misc_taken[bank], 1)
                if kind == "scores_exp":
                    grp = job * NG + g
                    u, bank = st["u"], unit % 2
                    if grp >= 3 and u == 0:
                        act.wait_ge(v_full, grp - 2)
                    act.wait_ge(b_full, unit + 1)
                    if s == 0 and u < 2:
                        dst = E[:, grp % 3, 2 * u:2 * u + 2, 0, :]
                    elif s == 0:
                        dst = E[:, grp % 3, :, 1, P:S]
                    else:
                        dst = E[:, grp % 3, 2 * (u % 2):2 * (u % 2) + 2, u // 2, :]
                    act.activation(dst, psB[:, bank].rearrange("p (h q) -> p h q", h=dst.shape[1]), ACT.Exp,
                                   scale=SCALE).then_inc(b_taken, 1)
                if kind == "values" and st["u"] == 1:
                    grp = job * NG + g
                    act.wait_ge(v_full, grp + 1)
                    if g == 0 and job >= 2:
                        for bank, k in use[("o_turn", *divmod(job - 2, NB))]:
                            act.wait_ge(misc_full[bank], k)
                    act.activation(oT[:, job % 2, g, :], psV[:, grp % 2, 0:S], ACT.Copy).then_inc(v_taken, 1)
                if kind == "o_back":
                    bank, k = misc[0]
                    act.wait_ge(misc_full[bank], k)
                    act.activation(oNT[:, job % 2, :], psM[:, bank, 0:S], ACT.Copy).then_inc(misc_taken[bank], 1)
                if kind == "moe_up":
                    n = b * TOPK + s
                    if n >= 2:
                        act.wait_ge(down_done, n - 1)
                    ps = (psA, psB)[n % 2]
                    for c in range(NC):
                        if c % 2 == 0:
                            act.wait_ge(up_full, 2 * n + c // 2 + 1)
                        act.activation(hid[:, n % 2, c, :], ps[:, c // 2, (c % 2) * S:(c % 2 + 1) * S], ACT.Gelu,
                                       bias=b1pick[:, b, s, c:c + 1]).then_inc(gelu_done, 1)

        @block.tensor
        def _(pe):
            def misc_free(bank, k):
                if k > 1:
                    pe.wait_ge(misc_taken[bank], k - 1)

            def taken(kind, s, b):
                for bank, k in use[(kind, s, b)]:
                    pe.wait_ge(misc_taken[bank], k)

            def turn(src, bank):
                for t in range(NT):
                    last = pe.transpose(psM[:, bank, t * P:(t + 1) * P], src[:, t, :], ident[:, :])
                return last

            V_BIAS = 2
            for st in steps:
                kind, s, b, g, misc, unit = st["kind"], st["s"], st["b"], st["g"], st["misc"], st["unit"]
                job = s * NB + b
                for bank, k in misc[:1]:
                    misc_free(bank, k)
                bank, k = misc[0] if misc else (0, 0)
                if kind == "ln_turn":
                    if s == 0 and b == 0:
                        pe.wait_ge(ident_set, 1)
                    pe.wait_ge(xn_ready, st["norm"] + 1)
                    turn(xn[:, b], bank).then_inc(misc_full[bank], 1)
                if kind == "qk_self":
                    if b == 0:
                        pe.wait_ge(wS_in, 16)
                    taken("ln_turn", 0, b)
                    for i, (bank, k) in enumerate(misc):
                        misc_free(bank, k)
                        for a in range(2):
                            last = pe.matmul(psM[:, bank, a * S:(a + 1) * S], wS[:, 2 * i + a, :], xnT[:, b, :],
                                             start=True, stop=True)
                        last.then_inc(misc_full[bank], 1)
                if kind == "v_self":
                    for t in range(NT):
                        last = pe.matmul(psM[:, bank, t * P:(t + 1) * P], xnT[:, b, t * P:(t + 1) * P], wS[:, 4, :],
                                         start=True, stop=True)
                    last.then_inc(misc_full[bank], 1)
                    if b == 0:
                        pe.wait_ge(rows_in, 32)
                        pe.transpose(psV[:, 0, 0:NE * NC], b1rows[:, :], ident[0:NE * NC, 0:NE * NC])
                        pe.transpose(psV[:, 0, NE * NC:NE * NC + NE], b2rows[:, :],
                                     ident[0:NE, 0:NE]).then_inc(bias_turned, 1)
                if kind == "ctx_turn":
                    if b == 0:
                        pe.wait_ge(ctx_loaded, 16)
                    turn(ctx_tok[:, b], bank).then_inc(misc_full[bank], 1)
                if kind == "k_cross":
                    if b == 0:
                        pe.wait_ge(wC_in, 16)
                    taken("ctx_turn", 1, b)
                    pe.matmul(psM[:, bank, 0:S], wC[:, 1, :], ctxT[:, b, :], start=True,
                              stop=True).then_inc(misc_full[bank], 1)
                if kind == "v_cross":
                    for t in range(NT):
                        last = pe.matmul(psM[:, bank, t * P:(t + 1) * P], ctxT[:, b, t * P:(t + 1) * P], wC[:, 2, :],
                                         start=True, stop=True)
                    last.then_inc(misc_full[bank], 1)
                if kind == "q_cross":
                    taken("ln_turn", 1, b)
                    pe.matmul(psM[:, bank, 0:S], wC[:, 0, :], xnT[:, b, :], start=True,
                              stop=True).then_inc(misc_full[bank], 1)
                if kind == "scores_max":
                    u, bank = st["u"], unit % 2
                    if unit == 0:
                        pe.wait_ge(consts, 6)
                    if g == 0 and u == 0:
                        pe.wait_ge(q_in[b], 16 * NPART * (s + 1))
                        pe.wait_ge(k_in[b], 16 * NPART * (s + 1))
                    if unit >= 2:
                        pe.wait_ge(a_taken, unit - 1)
                    if s == 0 and u == 0:
                        heads, t, keys = range(g * GH, (g + 1) * GH), 0, P
                    elif s == 0:
                        heads, t, keys = range(g * GH + 2 * (u - 1), g * GH + 2 * u), 1, S
                    else:
                        heads, t, keys = range(g * GH + 2 * (u % 2), g * GH + 2 * (u % 2) + 2), u // 2, S
                    for i, h in enumerate(heads):
                        last = pe.matmul(psA[:, bank, i * keys:(i + 1) * keys], stackQ[0:ROWS, b, h, t * P:(t + 1) * P],
                                         stackK[0:ROWS, b, h, 0:keys], start=(s == 1 or i == 0), stop=(s == 1),
                                         skip_group_check=True)
                    if s == 0:
                        blocks = psA[:, bank].rearrange("p (h k) -> p h k", h=len(heads))[:, :, keys - P:keys]
                        last = pe.matmul(blocks, ident16[:, :], mask16[:, 0:len(heads), :], start=False, stop=True,
                                         skip_group_check=True)
                    last.then_inc(a_full, 1)
                if kind == "max_rows":
                    pe.wait_ge(a_taken, a_units_until(job))
                    pe.transpose(psM[0:NT * NH, bank, 0:P], negmax[:, b, :], ident[:, :]).then_inc(misc_full[bank], 1)
                if kind == "scores_exp":
                    u, bank = st["u"], unit % 2
                    if g == 0 and u == 0:
                        pe.wait_ge(maxrow_in[b], 64 * (s + 1))
                    if unit >= 2:
                        pe.wait_ge(b_taken, unit - 1)
                    if s == 0 and u < 2:
                        heads, t, q0 = range(g * GH + 2 * u, g * GH + 2 * u + 2), 0, 0
                    elif s == 0:
                        heads, t, q0 = range(g * GH, (g + 1) * GH), 1, P
                    else:
                        heads, t, q0 = range(g * GH + 2 * (u % 2), g * GH + 2 * (u % 2) + 2), u // 2, 0
                    n = S - q0
                    for i, h in enumerate(heads):
                        last = pe.matmul(psB[:, bank, i * n:(i + 1) * n], stackK[:, b, h, t * P:(t + 1) * P],
                                         stackQ[:, b, h, q0:S], start=(s == 1 or i == 0), stop=(s == 1),
                                         skip_group_check=True)
                    if s == 0:
                        blocks = psB[:, bank].rearrange("p (h q) -> p h q", h=len(heads))[:, :, 0:P]
                        last = pe.matmul(blocks, ident16[:, :], mask16T[:, 0:len(heads), :], start=False, stop=True,
                                         skip_group_check=True)
                    last.then_inc(b_full, 1)
                if kind == "values":
                    grp, t = job * NG + g, st["u"]
                    if t == 0:
                        if grp == 0:
                            pe.wait_ge(v_taken, V_BIAS)
                        if grp >= 2:
                            pe.wait_ge(v_taken, V_BIAS + grp - 1)
                        if g == 0:
                            taken("v_self" if s == 0 else "v_cross", s, b)
                        pe.wait_ge(b_taken, b_units_until(grp))
                    q0 = P if s == 0 and t == 1 else 0
                    for i in range(GH):
                        last = pe.matmul(psV[i * VW:(i + 1) * VW, grp % 2, q0:S], V[:, b, t, g * GH + i, :],
                                         E[:, grp % 3, i, t, q0:S], start=(t == 0), stop=(t == 1),
                                         skip_group_check=True, tile_position=(0, i * VW))
                    if t == 1:
                        last.then_inc(v_full, 1)
                if kind == "o_turn":
                    pe.wait_ge(v_taken, V_BIAS + NG * (job + 1))
                    for t, (bank, k) in enumerate(misc):
                        misc_free(bank, k)
                        for i in range(NG):
                            last = pe.transpose(psM[:, bank, i * P:(i + 1) * P], oT[:, job % 2, i, t * P:(t + 1) * P],
                                                ident[:, :])
                        last.then_inc(misc_full[bank], 1)
                if kind == "o_back":
                    taken("o_turn", s, b)
                    turn(oN[:, job % 2], bank).then_inc(misc_full[bank], 1)
                if kind == "o_proj":
                    taken("o_back", s, b)
                    w = wS[:, 5, :] if s == 0 else wC[:, 3, :]
                    for t in range(NT):
                        last = pe.matmul(psM[:, bank, t * P:(t + 1) * P], oNT[:, job % 2, t * P:(t + 1) * P], w,
                                         start=True, stop=True)
                    last.then_inc(misc_full[bank], 1)
                if kind == "route":
                    if b == 0:
                        pe.wait_ge(gate_in, 16)
                    pe.wait_ge(seqrep, b + 1)
                    pe.matmul(psM[:, bank, 0:NE], xn[:, b, 0, :], gate_sb[:, :], start=True,
                              stop=True).then_inc(misc_full[bank], 1)
                if kind == "moe_up":
                    n = b * TOPK + s
                    if n == 0:
                        taken("ln_turn", 2, b)
                        pe.wait_ge(a_taken, a_total)
                        pe.wait_ge(b_taken, b_total)
                    if n >= 2:
                        pe.wait_ge(gelu_done, NC * (n - 1))
                    pe.wait_ge(w1_in[n % NW], 16 * (n // NW + 1))
                    ps = (psA, psB)[n % 2]
                    for c in range(NC):
                        last = pe.matmul(ps[:, c // 2, (c % 2) * S:(c % 2 + 1) * S],
                                         w1s[:, n % NW, c * P:(c + 1) * P], xnT[:, b, :], start=True, stop=True)
                        if c % 2:
                            last.then_inc(up_full, 1)
                if kind == "moe_down":
                    n = b * TOPK + s
                    if n == 0:
                        pe.wait_ge(v_taken, V_BIAS + NJOB * NG)
                    if s == 0 and b >= 2:
                        pe.wait_ge(y_taken, b - 1)
                    pe.wait_ge(w2_scaled, n + 1)
                    for c in range(NC):
                        pe.wait_ge(gelu_done, NC * n + c + 1)
                        last = pe.matmul(psV[:, b % 2, 0:S], w2s[:, n % NW, c, :], hid[:, n % 2, c, :],
                                         start=(s == 0 and c == 0), stop=(s == TOPK - 1 and c == NC - 1),
                                         skip_group_check=True)
                    last.then_inc(down_done, 1)
                if kind == "moe_out":
                    pe.wait_ge(y_taken, b + 1)
                    for t in range(NT):
                        last = pe.transpose(psM[:, bank, t * P:(t + 1) * P], yT[:, t * P:(t + 1) * P], ident[:, :])
                    last.then_inc(misc_full[bank], 1)


ONES16 = 1.0 + 0x3F80 * 2.0 ** -23


def kernel(x, ctx_1024, L0_attn_Wq, L0_attn_Wk, L0_attn_Wv, L0_attn_Wo, L0_xattn_W_kv, L0_xattn_W_q,
           L0_xattn_W_proj, L0_xattn_b_proj, L0_ffn_gate_w, L0_ffn_w1, L0_ffn_b1, L0_ffn_w2, L0_ffn_b2):
    import numpy as np
    import concourse.bacc as bacc
    from concourse.bass_utils import run_bass_kernel_spmd as run

    by_dim = np.arange(NH * HD).reshape(NH, HD).T.reshape(-1)
    turned = np.roll(np.arange(NH * HD).reshape(NH, HD), HD // 2, axis=1).T.reshape(-1)
    wq, wk = np.asarray(L0_attn_Wq), np.asarray(L0_attn_Wk)
    w_self = np.stack([wq[by_dim].T, wk[by_dim].T, wq[turned].T, wk[turned].T,
                       np.asarray(L0_attn_Wv).T, np.asarray(L0_attn_Wo).T], axis=1)
    kv = np.asarray(L0_xattn_W_kv)
    w_cross = np.stack([np.asarray(L0_xattn_W_q)[:, by_dim], kv[:, :D][:, by_dim], kv[:, D:],
                        np.asarray(L0_xattn_W_proj)], axis=1)
    freq = np.float32(1.0) / np.float32(10000.0) ** (np.arange(0, HD, 2, dtype=np.float32) / np.float32(HD))
    angle = np.outer(np.arange(S, dtype=np.float32), freq.astype(np.float32)).astype(np.float32)
    angle = np.concatenate([angle, angle], axis=1).T
    sign = np.where(np.arange(HD) < HD // 2, -1.0, 1.0).astype(np.float32)[:, None]
    rope = np.stack([np.repeat(np.cos(angle), NH, axis=0), np.repeat(np.sin(angle) * sign, NH, axis=0)], axis=1)

    arrays = {
        "x_dram": x, "ctx_dram": ctx_1024, "w_self_dram": w_self, "w_cross_dram": w_cross,
        "b_proj_dram": np.asarray(L0_xattn_b_proj), "rope_dram": rope.astype(np.float32), "gate_dram": L0_ffn_gate_w,
        "w1_dram": L0_ffn_w1, "b1_dram": L0_ffn_b1, "w2_dram": L0_ffn_w2, "b2_dram": L0_ffn_b2,
    }
    arrays = {k: np.ascontiguousarray(v) for k, v in arrays.items()}
    nc = bacc.Bacc("TRN2", target_bir_lowering=False, num_devices=1)
    args = [nc.dram_tensor(k, v.shape, mybir.dt.from_np(v.dtype), kind="ExternalInput").ap() for k, v in arrays.items()]
    out = nc.dram_tensor("out_dram", (NB, S, D), F32, kind="ExternalOutput").ap()
    build(nc, *args, out)
    r = run(nc, [arrays], core_ids=[0])
    return r.results[0]["out_dram"]
```

```python
from contextlib import ExitStack

import concourse.bass as bass
from concourse import mybir

ALU = mybir.AluOpType
ACT = mybir.ActivationFunctionType
AX_X = mybir.AxisListType.X
F32 = mybir.dt.float32
BF16 = mybir.dt.bfloat16
U32 = mybir.dt.uint32

NB, S, D = 4, 256, 128
P = 128
NT = S // P
NH, HD = 16, 8
NG, GH = 4, 4
NE, TOPK, FF = 8, 2, 512
NC = FF // P
NPART = 3
ROWS = 96
MAXROW = 96
VW = 32
SCALE = float(HD) ** -0.5
EPS = 1e-5
MASKED = -2.0 ** 100
LAG = 6
NJOB = 2 * NB
GRP_UNITS = (3, 4)


def plan():
    before, after_a, after_b = {}, {}, {}

    def put(where, n, *step):
        where.setdefault(n, []).append(step)

    start = [("ln_stats", 0, 0), ("ln_apply", 0, 0), ("ln_turn", 0, 0), ("ln_stats", 0, 1), ("init_stack", 0, 0),
             ("ln_apply", 0, 1), ("constants", 0, 0), ("qk_self", 0, 0), ("ln_turn", 0, 1), ("stack_write", 0, 0),
             ("ln_stats", 0, 2), ("ln_stats", 0, 3),
             ("stack_read", 0, 0), ("init_v", 0, 0), ("v_self", 0, 0), ("qk_self", 0, 1),
             ("ln_apply", 0, 2), ("ln_apply", 0, 3), ("ln_turn", 0, 2), ("ln_turn", 0, 3), ("init_stack", 0, 1),
             ("stack_write", 0, 1), ("stack_read", 0, 1), ("init_v", 0, 1)]
    for b in (2, 3):
        n = 4 * b - 8
        put(after_b, n + 1, "qk_self", 0, b)
        put(after_b, n + 3, "init_stack", 0, b)
        put(after_b, n + 4, "stack_write", 0, b)
        put(after_b, n + 5, "stack_read", 0, b)
        put(after_b, n + 6, "init_v", 0, b)
    for b in range(1, NB):
        put(after_b, 4 * b, "v_self", 0, b)
    for j in range(NJOB):
        s, b = divmod(j, NB)
        n = 4 * j
        put(after_a, n + 4, "max_rows", s, b)
        put(after_a, n + 11, "o_turn", s, b)
        put(after_b, n + 11, "o_back", s, b)
        put(after_a, n + 12, "o_proj", s, b)
        put(after_a, n + 12, "ln_stats", s + 1, b)
        put(after_b, n + 12, "ln_apply", s + 1, b)
        put(after_a, n + 13, "ln_turn", s + 1, b)
        if s == 0:
            put(after_b, n + 9, "ctx_turn", 1, b)
            put(after_a, n + 10, "k_cross", 1, b)
            put(after_b, n + 12, "stack_write_k", 1, b)
            put(after_b, n + 12, "v_cross", 1, b)
            put(after_a, n + 13, "stack_read_k", 1, b)
            put(after_b, n + 13, "q_cross", 1, b)
            put(after_b, n + 13, "stack_write", 1, b)
            put(after_b, n + 14, "stack_read", 1, b)
        else:
            put(after_b, n + 13, "route_mean", 2, b)
            put(after_a, n + 14, "route", 2, b)
            put(after_b, n + 14, "route_pick", 2, b)
    ffn = [("moe_up", 0), ("moe_up", 1), ("moe_down", 0)]
    for n in range(2, 2 * NB):
        ffn += [("moe_up", n), ("moe_down", n - 1)]
        if n % 2 == 0:
            ffn.append(("moe_out", n - 1))
    ffn += [("moe_down", 2 * NB - 1), ("moe_out", 2 * NB - 1)]
    for n, k in ((38, 3), (39, 2), (40, 3), (41, 3)):
        for f in ffn[:k]:
            put(after_b, n, f[0], f[1] % 2, f[1] // 2)
        del ffn[:k]

    order = list(start)
    for n in range(NJOB * NG + 12):
        halves = [[], []]
        for kind, m in (("scores_max", n), ("scores_exp", n - LAG)):
            if 0 <= m < NJOB * NG:
                s, b = divmod(m // NG, NB)
                for u in range(GRP_UNITS[s]):
                    halves[u // 2].append((u, (kind, s, b, m % NG, u)))
        for half, extra in zip(range(2), (after_a, after_b)):
            order += [step for _, step in sorted(halves[half])]
            m = n - LAG - 1
            if 0 <= m < NJOB * NG:
                order.append(("values", *divmod(m // NG, NB), m % NG, half))
            order += extra.get(n, [])
    order += [(f[0], f[1] % 2, f[1] // 2) for f in ffn]

    uses = {"ln_turn": 1, "qk_self": 2, "v_self": 1, "ctx_turn": 1, "k_cross": 1, "v_cross": 1, "q_cross": 1,
            "max_rows": 1, "o_turn": 2, "o_back": 1, "o_proj": 1, "route": 1}
    count, total, steps = [0, 0], 0, []
    a_unit = b_unit = 0
    norms = {}
    for kind, s, b, *g in order:
        misc = []
        for _ in range(uses.get(kind, 0)):
            bank = total % 2
            count[bank] += 1
            misc.append((bank, count[bank]))
            total += 1
        st = dict(kind=kind, s=s, b=b, g=g[0] if g else 0, u=g[1] if g else 0, misc=misc, unit=0, norm=norms.get(kind, 0))
        if kind == "scores_max":
            st["unit"] = a_unit
            a_unit += 1
        if kind == "scores_exp":
            st["unit"] = b_unit
            b_unit += 1
        norms[kind] = norms.get(kind, 0) + 1
        steps.append(st)
    return steps, a_unit, b_unit


def a_units_until(job):
    return sum(NG * GRP_UNITS[j // NB] for j in range(job + 1))


def b_units_until(group):
    return sum(GRP_UNITS[n // (NG * NB)] for n in range(group + 1))


def build(nc, x, ctx_in, w_self, w_cross, b_proj, rope, gate_w, w1_biases, w2, out):
    steps, a_total, b_total = plan()
    use = {(st["kind"], st["s"], st["b"]): st["misc"] for st in steps if st["misc"]}

    scratch_q = nc.dram_tensor("scratch_q", [2, NB, NPART, P, S], BF16).ap()
    scratch_k = nc.dram_tensor("scratch_k", [2, NB, NPART, P, S], BF16).ap()

    with ExitStack() as ctx:
        def sb(name, shape, dt=F32):
            return ctx.enter_context(nc.sbuf_tensor(name, shape, dt))

        def sem(name):
            return ctx.enter_context(nc.semaphore(name))

        def sems(name, n=NB):
            return [sem(f"{name}{i}") for i in range(n)]

        res = sb("res", [P, NB, NT, D])
        ctx_tok = sb("ctx_tok", [P, NB, NT, D])
        wS = sb("wS", [P, 6, D])
        wC = sb("wC", [P, 4, D])
        gate_sb = sb("gate_sb", [P, NE])
        rope_sb = sb("rope_sb", [P, 2, S])
        bproj = sb("bproj", [P, D])
        ident = sb("ident", [P, P])
        ident16 = sb("ident16", [P, P], BF16)
        mask16 = sb("mask16", [P, GH, P], BF16)
        mask16T = sb("mask16T", [P, GH, P], BF16)
        ones = sb("ones", [P, P])
        neg_half = sb("neg_half", [P, NT])
        euler = sb("euler", [P, NE])
        stats = sb("stats", [P, NB, NT, 6])
        mv = sb("mv", [P, NB, NT, 2])
        rstd = sb("rstd", [P, NB, NT])
        xn = sb("xn", [P, NB, NT, D])
        xnT = sb("xnT", [P, NB, S])
        ctxT = sb("ctxT", [P, NB, S])
        rot = sb("rot", [P, 2, 2, 2, S])
        kc = sb("kc", [P, 2, S])
        parts = sb("parts", [P, NB, 2, NPART, S], BF16)
        stackQ = sb("stackQ", [MAXROW + 2, NB, NH, S], BF16)
        stackK = sb("stackK", [MAXROW + 2, NB, NH, S], BF16)
        V = sb("V", [P, NB, NT, NH, VW])
        negmax = sb("negmax", [P, NB, NT * NH])
        maxT = sb("maxT", [NT * NH, NB, 2, P], BF16)
        E = sb("E", [P, 3, GH, NT, S])
        oT = sb("oT", [P, 2, NG, S])
        rden = sb("rden", [P, 2, NT, NH])
        oN = sb("oN", [P, 2, NT, D])
        oNT = sb("oNT", [P, 2, S])
        seqsum = sb("seqsum", [P, NB, 1])
        small = sb("small", [P, NB, 8, NE])
        top_i = sb("top_i", [P, NB, NE], U32)
        b2row = sb("b2row", [1, NB, TOPK, D])
        NW = 4
        w1s = sb("w1s", [P, NW, FF + NC])
        w2s = sb("w2s", [P, NW, NC, D])
        hid = sb("hid", [P, 2, NC, S])

        psA = ctx.enter_context(nc.psum_tensor("psA", [P, 2, 512], F32))
        psB = ctx.enter_context(nc.psum_tensor("psB", [P, 2, 512], F32))
        psV = ctx.enter_context(nc.psum_tensor("psV", [P, 2, 512], F32))
        psM = ctx.enter_context(nc.psum_tensor("psM", [P, 2, 512], F32))

        x_in, ctx_loaded = sems("x_in"), sem("ctx_loaded")
        wS_in, wC_in, rope_in = sem("wS_in"), sem("wC_in"), sem("rope_in")
        gate_in, bproj_in = sem("gate_in"), sem("bproj_in")
        ident_set, consts, stack_init, v_init = sem("ident_set"), sem("consts"), sems("stack_init"), sem("v_init")
        misc_full, misc_taken = sems("misc_full", 2), sems("misc_taken", 2)
        var_ready, rstd_ready, xn_ready = sem("var_ready"), sem("rstd_ready"), sem("xn_ready")
        parts_self, parts_k, parts_q = sems("parts_self"), sems("parts_k"), sems("parts_q")
        scr_q, scr_k = sems("scr_q"), sems("scr_k")
        q_in, k_in, maxrow_in = sems("q_in"), sems("k_in"), sems("maxrow_in")
        a_full, a_taken = sem("a_full"), sem("a_taken")
        b_full, b_taken = sem("b_full"), sem("b_taken")
        v_full, v_taken = sem("v_full"), sem("v_taken")
        oN_ready = sem("oN_ready")
        probs_ready = sem("probs_ready")
        seqrep = sem("seqrep")
        chosen, weights_ready = sem("chosen"), sem("weights_ready")
        b2_in, b2_scaled = sems("b2_in"), sem("b2_scaled")
        w1_in, w2_in, w2_scaled = sems("w1_in", NW), sems("w2_in", NW), sem("w2_scaled")
        up_full, gelu_done, down_done = sem("up_full"), sem("gelu_done"), sem("down_done")
        y_taken = sem("y_taken")
        stored = sem("stored")
        dve_own, pool_own, act_own = sem("dve_own"), sem("pool_own"), sem("act_own")

        block = ctx.enter_context(nc.Block())

        @block.sync
        def _(sp):
            for b in range(NB):
                sp.dma_start(res[:, b], x[b].rearrange("(t p) d -> p t d", p=P)).then_inc(x_in[b], 16)
                if b == 0:
                    sp.dma_start(wS[:, :, :], w_self).then_inc(wS_in, 16)
                    sp.dma_start(rope_sb[:, :, :], rope).then_inc(rope_in, 16)
            sp.dma_start(ctx_tok[:, :, :, :],
                         ctx_in.rearrange("b (t p) d -> p (b t) d", p=P)).then_inc(ctx_loaded, 16)
            sp.dma_start(wC[:, :, :], w_cross).then_inc(wC_in, 16)
            sp.dma_start(gate_sb[:, :], gate_w).then_inc(gate_in, 16)
            sp.dma_start(bproj[:, :], b_proj.partition_broadcast(P)).then_inc(bproj_in, 16)

            def write_parts(s, b, which, scratch, done):
                sp.dma_start(scratch[s, b].rearrange("i p t -> p i t"),
                             parts[:, b, which]).then_inc(done, 16)

            def read_q(s, b):
                sp.wait_ge(scr_q[b], 16 * (s + 1))
                for i in range(NPART):
                    r = i * NPART * HD
                    src = scratch_q[s, b, i]
                    thrice = bass.AP(src.tensor, src.offset, [[0, NPART], [NH * S, HD], [1, NH * S]])
                    sp.dma_start(stackQ[r:r + NPART * HD, b], thrice).then_inc(q_in[b], 16)

            def read_k(s, b):
                sp.wait_ge(scr_k[b], 16 * (s + 1))
                for i in range(NPART):
                    r = i * NPART * HD
                    sp.dma_start(stackK[r:r + NPART * HD, b],
                                 scratch_k[s, b].rearrange("i (d h) t -> (i d) h t", h=NH)).then_inc(k_in[b], 16)

            expert = 0
            for st in steps:
                kind, s, b = st["kind"], st["s"], st["b"]
                if kind == "stack_write" and s == 0:
                    sp.wait_ge(parts_self[b], 1)
                    write_parts(s, b, 1, scratch_k, scr_k[b])
                    write_parts(s, b, 0, scratch_q, scr_q[b])
                if kind == "stack_read" and s == 0:
                    sp.wait_ge(stack_init[b], 2)
                    read_k(s, b)
                    read_q(s, b)
                if kind == "stack_write_k":
                    sp.wait_ge(parts_k[b], 1)
                    write_parts(s, b, 1, scratch_k, scr_k[b])
                if kind == "stack_read_k":
                    sp.wait_ge(b_full, b_units_until(NG * (b + 1) - 1))
                    read_k(s, b)
                if kind == "stack_write" and s == 1:
                    sp.wait_ge(parts_q[b], 1)
                    write_parts(s, b, 0, scratch_q, scr_q[b])
                if kind == "stack_read" and s == 1:
                    read_q(s, b)
                if kind == "max_rows":
                    sp.wait_ge(misc_taken[st["misc"][0][0]], st["misc"][0][1])
                    for i in range(2):
                        for t in range(NT):
                            sp.dma_start(stackQ[MAXROW + i:MAXROW + i + 1, b, :, t * P:(t + 1) * P],
                                         maxT[t * NH:(t + 1) * NH, b, i, :]).then_inc(maxrow_in[b], 16)
                if kind == "route_pick":
                    sp.wait_ge(chosen, b + 1)
                    for k in range(TOPK):
                        n = b * TOPK + k
                        e = sp.value_load(top_i[0:1, b, k:k + 1], min_val=0, max_val=NE - 1)
                        if n >= NW:
                            sp.wait_ge(down_done, n - NW + 1)
                        sp.dma_start(w1s[:, n % NW, :],
                                     w1_biases[bass.ds(e, 1), 0:P].rearrange("e p f -> p (e f)")).then_inc(w1_in[n % NW], 16)
                        sp.dma_start(w2s[:, n % NW, :, :],
                                     w2[bass.ds(e, 1), 0:FF].rearrange("e (c p) d -> p (e c) d", p=P)).then_inc(w2_in[n % NW], 16)
                        sp.dma_start(b2row[:, b, k, :],
                                     w2[bass.ds(e, 1), FF:FF + 1].rearrange("e o d -> (e o) d")).then_inc(b2_in[b], 16)
                if kind == "moe_out":
                    sp.wait_ge(y_taken, b + 1)
                    sp.dma_start(out[b].rearrange("(t p) d -> p t d", p=P), res[:, b]).then_inc(stored, 16)
            sp.wait_ge(stored, 16 * NB)

        @block.gpsimd
        def _(pool):
            own = [0]

            def then(ins):
                own[0] += 1
                ins.then_inc(pool_own, 1)
                pool.wait_ge(pool_own, own[0])

            def split(src, dst, ready):
                then(pool.tensor_copy(dst[:, :, 0], src))
                then(pool.tensor_tensor(src, src, dst[:, :, 0], ALU.subtract))
                then(pool.tensor_copy(dst[:, :, 1], src))
                pool.tensor_tensor(dst[:, :, 2], src, dst[:, :, 1], ALU.subtract).then_inc(ready, 1)

            def constants():
                pool.memset(ones[:, :], 1.0).then_inc(consts, 1)
                pool.memset(euler[:, :], 2.718281828459045).then_inc(consts, 1)
                then(pool.memset(ident16[:, :], 0.0))
                pool.affine_select(out=ident16[:, :], in_=ident16[:, :], compare_op=ALU.not_equal, fill=1.0, base=0,
                                   pattern=[[-1, P]], channel_multiplier=1).then_inc(consts, 1)
                for m, sign in ((mask16, 1), (mask16T, -1)):
                    then(pool.memset(m[:, :, :], 0.0))
                    pool.affine_select(out=m[:, :, :], in_=m[:, :, :], compare_op=ALU.is_ge, fill=MASKED, base=0,
                                       pattern=[[0, GH], [-sign, P]], channel_multiplier=sign).then_inc(consts, 1)

            then(pool.memset(neg_half[:, :], -0.5))
            then(pool.memset(ident[:, :], 0.0))
            pool.affine_select(out=ident[:, :], in_=ident[:, :], compare_op=ALU.not_equal, fill=1.0, base=0,
                               pattern=[[-1, P]], channel_multiplier=1).then_inc(ident_set, 1)

            def init_v(b):
                then(pool.memset(V[:, b], 0.0))
                pool.memset(V[:, b, :, :, HD:HD + 1], 1.0).then_inc(v_init, 1)
                pool.wait_ge(v_init, b + 1)

            def init_stack(b):
                pool.memset(stackQ[0:ROWS, b].bitcast(F32), 0.0).then_inc(stack_init[b], 1)
                pool.memset(stackK[:, b].bitcast(F32), ONES16).then_inc(stack_init[b], 1)

            def rsqrt_var(n, b):
                pool.wait_ge(var_ready, n + 1)
                then(pool.tensor_scalar(rstd[:, b, :], mv[:, b, :, 1], EPS, None, ALU.add))
                pool.tensor_tensor(rstd[:, b, :], rstd[:, b, :], neg_half[:, :], ALU.pow).then_inc(rstd_ready, 1)
                pool.wait_ge(rstd_ready, n + 1)

            for st in steps:
                kind, s, b, misc, unit = st["kind"], st["s"], st["b"], st["misc"], st["unit"]
                if kind == "ln_stats":
                    rsqrt_var(st["norm"], b)
                if kind == "constants":
                    constants()
                if kind == "init_v":
                    init_v(b)
                if kind == "init_stack":
                    init_stack(b)
                if kind == "qk_self" and b >= 1:
                    for bank, k in misc:
                        pool.wait_ge(misc_taken[bank], k)
                    cs, sn = rot[:, b % 2, 0], rot[:, b % 2, 1]
                    then(pool.tensor_tensor(cs, cs, sn, ALU.add))
                    split(cs, parts[:, b], parts_self[b])
                if kind == "k_cross":
                    bank, k = misc[0]
                    pool.wait_ge(misc_taken[bank], k)
                    kk = kc[:, b % 2:b % 2 + 1]
                    split(kk, parts[:, b, 1:2], parts_k[b])
                if kind == "route":
                    bank, k = misc[0]
                    pool.wait_ge(misc_taken[bank], k)
                    pool.tensor_tensor(small[:, b, 1], euler[:, :], small[:, b, 0], ALU.pow).then_inc(probs_ready, 1)
                if kind == "moe_up":
                    n = b * TOPK + s
                    weight = small[:, b, 6, s:s + 1]
                    pool.wait_ge(weights_ready, b + 1)
                    if s == 0:
                        pool.wait_ge(b2_in[b], 16 * TOPK)
                        for k in range(TOPK):
                            pool.tensor_scalar(b2row[:, b, k], b2row[:, b, k], small[0:1, b, 6, k:k + 1], None,
                                               ALU.mult).then_inc(b2_scaled, 1)
                    pool.wait_ge(w2_in[n % NW], 16 * (n // NW + 1))
                    pool.tensor_scalar(w2s[:, n % NW], w2s[:, n % NW], weight, None, ALU.mult).then_inc(w2_scaled, 1)

        @block.vector
        def _(dve):
            own = [0]

            def then(ins):
                own[0] += 1
                ins.then_inc(dve_own, 1)
                dve.wait_ge(dve_own, own[0])

            def split(src, dst, ready):
                then(dve.tensor_copy(dst[:, :, 0], src))
                then(dve.tensor_tensor(src, src, dst[:, :, 0], ALU.subtract))
                then(dve.tensor_copy(dst[:, :, 1], src))
                dve.tensor_tensor(dst[:, :, 2], src, dst[:, :, 1], ALU.subtract).then_inc(ready, 1)

            for st in steps:
                kind, s, b, g, misc, unit = st["kind"], st["s"], st["b"], st["g"], st["misc"], st["unit"]
                job = s * NB + b
                if kind == "ln_stats":
                    if s == 0:
                        dve.wait_ge(x_in[b], 16)
                    for t in range(NT):
                        last = dve.bn_stats(stats[:, b, t, :], res[:, b, t, :])
                        if t == NT - 1:
                            then(last)
                    for t in range(NT):
                        last = dve.bn_aggr(mv[:, b, t, :], stats[:, b, t, :])
                    last.then_inc(var_ready, 1)
                if kind == "ln_apply":
                    dve.wait_ge(rstd_ready, st["norm"] + 1)
                    for t in range(NT):
                        last = dve.tensor_scalar(xn[:, b, t, :], res[:, b, t, :], mv[:, b, t, 0:1], rstd[:, b, t:t + 1],
                                                 ALU.subtract, ALU.mult)
                    last.then_inc(xn_ready, 1)
                if kind == "qk_self":
                    if b == 0:
                        dve.wait_ge(rope_in, 16)
                    if b == 3:
                        dve.wait_ge(parts_self[b - 2], 1)
                    for i, (bank, k) in enumerate(misc):
                        dve.wait_ge(misc_full[bank], k)
                        table = rope_sb[:, i:i + 1, :].to_broadcast([P, 2, S])
                        dve.tensor_tensor(rot[:, b % 2, i], psM[:, bank].rearrange("p (a t) -> p a t", a=2), table,
                                          ALU.mult).then_inc(misc_taken[bank], 1)
                    if b == 0:
                        for bank, k in misc:
                            dve.wait_ge(misc_taken[bank], k)
                        cs = rot[:, b % 2, 0]
                        then(dve.tensor_tensor(cs, cs, rot[:, b % 2, 1], ALU.add))
                        split(cs, parts[:, b], parts_self[b])
                if kind == "q_cross":
                    bank, k = misc[0]
                    dve.wait_ge(misc_full[bank], k)
                    qq, dst = rot[:, b % 2, 0, 0], parts[:, b, 0]
                    then(dve.tensor_copy(dst[:, 0], psM[:, bank, 0:S]))
                    dve.tensor_tensor(qq, psM[:, bank, 0:S], dst[:, 0], ALU.subtract).then_inc(misc_taken[bank], 1)
                    dve.wait_ge(misc_taken[bank], k)
                    then(dve.tensor_copy(dst[:, 1], qq))
                    dve.tensor_tensor(dst[:, 2], qq, dst[:, 1], ALU.subtract).then_inc(parts_q[b], 1)
                if kind == "scores_max":
                    u, bank = st["u"], unit % 2
                    dve.wait_ge(a_full, unit + 1)
                    if s == 0 and u == 0:
                        cols, nh = g * GH, GH
                    elif s == 0:
                        cols, nh = NH + g * GH + 2 * (u - 1), 2
                    else:
                        cols, nh = (u // 2) * NH + g * GH + 2 * (u % 2), 2
                    dve.tensor_reduce(negmax[:, b, cols:cols + nh], psA[:, bank].rearrange("p (h k) -> p h k", h=nh),
                                      AX_X, ALU.max, negate=True).then_inc(a_taken, 1)
                if kind == "max_rows":
                    bank, k = misc[0]
                    dve.wait_ge(misc_full[bank], k)
                    if s == 1:
                        dve.wait_ge(maxrow_in[b], 64)
                    m = psM[0:NT * NH, bank, 0:P]
                    then(dve.tensor_copy(maxT[:, b, 0, :], m))
                    dve.tensor_tensor(maxT[:, b, 1, :], m, maxT[:, b, 0, :], ALU.subtract).then_inc(misc_taken[bank], 1)
                if kind == "o_turn" and s == 1:
                    if b == 0:
                        dve.wait_ge(bproj_in, 16)
                    then(dve.tensor_tensor(res[:, b], res[:, b],
                                           bproj[:, :].rearrange("p (o d) -> p o d", o=1).to_broadcast([P, NT, D]),
                                           ALU.add))
                if kind == "o_turn":
                    for t, (bank, k) in enumerate(misc):
                        dve.wait_ge(misc_full[bank], k)
                        o = psM[:, bank].rearrange("p (h c) -> p h c", c=VW)
                        then(dve.reciprocal(rden[:, job % 2, t, :], o[:, :, HD]))
                        r = rden[:, job % 2, t, :].rearrange("p (h o) -> p h o", o=1).to_broadcast([P, NH, HD])
                        dve.tensor_tensor(oN[:, job % 2, t, :].rearrange("p (h c) -> p h c", c=HD), o[:, :, 0:HD], r,
                                          ALU.mult).then_inc(misc_taken[bank], 1)
                if kind == "o_proj":
                    bank, k = misc[0]
                    dve.wait_ge(misc_full[bank], k)
                    y = psM[:, bank, 0:S].rearrange("p (t d) -> p t d", t=NT)
                    dve.tensor_tensor(res[:, b], res[:, b], y, ALU.add).then_inc(misc_taken[bank], 1)
                    dve.wait_ge(misc_taken[bank], k)
                if kind == "route_mean":
                    turned = use[("ln_turn", 2, b)][0]
                    dve.wait_ge(misc_taken[turned[0]], turned[1])
                    dve.tensor_scalar(xn[:, b, 0, :], ones[:, :], seqsum[:, b, 0:1], 1.0 / S, ALU.mult,
                                      ALU.mult).then_inc(seqrep, 1)
                if kind == "route":
                    bank, k = misc[0]
                    dve.wait_ge(misc_full[bank], k)
                    v = small[:, b]
                    then(dve.tensor_reduce(v[:, 3, 0:1], psM[:, bank, 0:NE], AX_X, ALU.max))
                    dve.tensor_scalar(v[:, 0], psM[:, bank, 0:NE], v[:, 3, 0:1], None,
                                      ALU.subtract).then_inc(misc_taken[bank], 1)
                if kind == "route_pick":
                    v = small[:, b]
                    dve.wait_ge(probs_ready, b + 1)
                    then(dve.max(v[:, 4], v[:, 1]))
                    dve.max_index(top_i[:, b, :], v[:, 4], v[:, 1]).then_inc(chosen, 1)
                    then(dve.tensor_tensor(v[:, 5, 0:1], v[:, 4, 0:1], v[:, 4, 1:2], ALU.add))
                    then(dve.reciprocal(v[:, 5, 1:2], v[:, 5, 0:1]))
                    dve.tensor_scalar(v[:, 6, 0:TOPK], v[:, 4, 0:TOPK], v[:, 5, 1:2], None,
                                      ALU.mult).then_inc(weights_ready, 1)
                if kind == "moe_out":
                    dve.wait_ge(down_done, TOPK * (b + 1))
                    dve.tensor_tensor(res[:, b], res[:, b], psV[:, b % 2, 0:S].rearrange("p (t d) -> p t d", t=NT),
                                      ALU.add).then_inc(y_taken, 1)

        @block.scalar
        def _(act):
            for st in steps:
                kind, s, b, g, misc, unit = st["kind"], st["s"], st["b"], st["g"], st["misc"], st["unit"]
                job = s * NB + b
                if kind == "ln_turn":
                    bank, k = misc[0]
                    act.wait_ge(misc_full[bank], k)
                    if s < 2:
                        act.activation(xnT[:, b, :], psM[:, bank, 0:S], ACT.Copy).then_inc(misc_taken[bank], 1)
                    else:
                        act.activation(xnT[:, b, :], psM[:, bank, 0:S], ACT.Copy,
                                       accum_out=seqsum[:, b, 0:1]).then_inc(misc_taken[bank], 1)
                if kind == "ctx_turn":
                    bank, k = misc[0]
                    act.wait_ge(misc_full[bank], k)
                    act.activation(ctxT[:, b, :], psM[:, bank, 0:S], ACT.Copy).then_inc(misc_taken[bank], 1)
                if kind in ("v_self", "v_cross"):
                    bank, k = misc[0]
                    act.wait_ge(misc_full[bank], k)
                    if kind == "v_self":
                        act.wait_ge(v_init, b + 1)
                    else:
                        act.wait_ge(v_full, NG * (b + 1))
                    act.activation(V[:, b, :, :, 0:HD],
                                   psM[:, bank, 0:S].rearrange("p (t h d) -> p t h d", t=NT, h=NH),
                                   ACT.Copy).then_inc(misc_taken[bank], 1)
                if kind == "k_cross":
                    bank, k = misc[0]
                    act.wait_ge(misc_full[bank], k)
                    if b >= 2:
                        act.wait_ge(parts_k[b - 2], 1)
                    act.activation(kc[:, b % 2], psM[:, bank, 0:S], ACT.Copy).then_inc(misc_taken[bank], 1)
                if kind == "scores_exp":
                    grp = job * NG + g
                    u, bank = st["u"], unit % 2
                    if grp >= 3 and u == 0:
                        act.wait_ge(v_full, grp - 2)
                    act.wait_ge(b_full, unit + 1)
                    if s == 0 and u < 2:
                        dst = E[:, grp % 3, 2 * u:2 * u + 2, 0, :]
                    elif s == 0:
                        dst = E[:, grp % 3, :, 1, P:S]
                    else:
                        dst = E[:, grp % 3, 2 * (u % 2):2 * (u % 2) + 2, u // 2, :]
                    act.activation(dst, psB[:, bank].rearrange("p (h q) -> p h q", h=dst.shape[1]), ACT.Exp,
                                   scale=SCALE).then_inc(b_taken, 1)
                if kind == "values" and st["u"] == 1:
                    grp = job * NG + g
                    act.wait_ge(v_full, grp + 1)
                    if g == 0 and job >= 2:
                        for bank, k in use[("o_turn", *divmod(job - 2, NB))]:
                            act.wait_ge(misc_full[bank], k)
                    act.activation(oT[:, job % 2, g, :], psV[:, grp % 2, 0:S], ACT.Copy).then_inc(v_taken, 1)
                if kind == "o_back":
                    bank, k = misc[0]
                    act.wait_ge(misc_full[bank], k)
                    act.activation(oNT[:, job % 2, :], psM[:, bank, 0:S], ACT.Copy).then_inc(misc_taken[bank], 1)
                if kind == "moe_up":
                    n = b * TOPK + s
                    if n >= 2:
                        act.wait_ge(down_done, n - 1)
                    ps = (psA, psB)[n % 2]
                    act.wait_ge(w1_in[n % NW], 16 * (n // NW + 1))
                    for c in range(NC):
                        if c % 2 == 0:
                            act.wait_ge(up_full, 2 * n + c // 2 + 1)
                        act.activation(hid[:, n % 2, c, :], ps[:, c // 2, (c % 2) * S:(c % 2 + 1) * S], ACT.Gelu,
                                       bias=w1s[:, n % NW, FF + c:FF + c + 1]).then_inc(gelu_done, 1)

        @block.tensor
        def _(pe):
            def misc_free(bank, k):
                if k > 1:
                    pe.wait_ge(misc_taken[bank], k - 1)

            def taken(kind, s, b):
                for bank, k in use[(kind, s, b)]:
                    pe.wait_ge(misc_taken[bank], k)

            def turn(src, bank):
                for t in range(NT):
                    last = pe.transpose(psM[:, bank, t * P:(t + 1) * P], src[:, t, :], ident[:, :])
                return last

            for st in steps:
                kind, s, b, g, misc, unit = st["kind"], st["s"], st["b"], st["g"], st["misc"], st["unit"]
                job = s * NB + b
                for bank, k in misc[:1]:
                    misc_free(bank, k)
                bank, k = misc[0] if misc else (0, 0)
                if kind == "ln_turn":
                    if s == 0 and b == 0:
                        pe.wait_ge(ident_set, 1)
                    pe.wait_ge(xn_ready, st["norm"] + 1)
                    turn(xn[:, b], bank).then_inc(misc_full[bank], 1)
                if kind == "qk_self":
                    if b == 0:
                        pe.wait_ge(wS_in, 16)
                    taken("ln_turn", 0, b)
                    for i, (bank, k) in enumerate(misc):
                        misc_free(bank, k)
                        for a in range(2):
                            last = pe.matmul(psM[:, bank, a * S:(a + 1) * S], wS[:, 2 * i + a, :], xnT[:, b, :],
                                             start=True, stop=True)
                        last.then_inc(misc_full[bank], 1)
                if kind == "v_self":
                    for t in range(NT):
                        last = pe.matmul(psM[:, bank, t * P:(t + 1) * P], xnT[:, b, t * P:(t + 1) * P], wS[:, 4, :],
                                         start=True, stop=True)
                    last.then_inc(misc_full[bank], 1)
                if kind == "ctx_turn":
                    if b == 0:
                        pe.wait_ge(ctx_loaded, 16)
                    turn(ctx_tok[:, b], bank).then_inc(misc_full[bank], 1)
                if kind == "k_cross":
                    if b == 0:
                        pe.wait_ge(wC_in, 16)
                    taken("ctx_turn", 1, b)
                    pe.matmul(psM[:, bank, 0:S], wC[:, 1, :], ctxT[:, b, :], start=True,
                              stop=True).then_inc(misc_full[bank], 1)
                if kind == "v_cross":
                    for t in range(NT):
                        last = pe.matmul(psM[:, bank, t * P:(t + 1) * P], ctxT[:, b, t * P:(t + 1) * P], wC[:, 2, :],
                                         start=True, stop=True)
                    last.then_inc(misc_full[bank], 1)
                if kind == "q_cross":
                    taken("ln_turn", 1, b)
                    pe.matmul(psM[:, bank, 0:S], wC[:, 0, :], xnT[:, b, :], start=True,
                              stop=True).then_inc(misc_full[bank], 1)
                if kind == "scores_max":
                    u, bank = st["u"], unit % 2
                    if unit == 0:
                        pe.wait_ge(consts, 5)
                    if g == 0 and u == 0:
                        pe.wait_ge(q_in[b], 16 * NPART * (s + 1))
                        pe.wait_ge(k_in[b], 16 * NPART * (s + 1))
                    if unit >= 2:
                        pe.wait_ge(a_taken, unit - 1)
                    if s == 0 and u == 0:
                        heads, t, keys = range(g * GH, (g + 1) * GH), 0, P
                    elif s == 0:
                        heads, t, keys = range(g * GH + 2 * (u - 1), g * GH + 2 * u), 1, S
                    else:
                        heads, t, keys = range(g * GH + 2 * (u % 2), g * GH + 2 * (u % 2) + 2), u // 2, S
                    for i, h in enumerate(heads):
                        last = pe.matmul(psA[:, bank, i * keys:(i + 1) * keys], stackQ[0:ROWS, b, h, t * P:(t + 1) * P],
                                         stackK[0:ROWS, b, h, 0:keys], start=(s == 1 or i == 0), stop=(s == 1),
                                         skip_group_check=True)
                    if s == 0:
                        blocks = psA[:, bank].rearrange("p (h k) -> p h k", h=len(heads))[:, :, keys - P:keys]
                        last = pe.matmul(blocks, ident16[:, :], mask16[:, 0:len(heads), :], start=False, stop=True,
                                         skip_group_check=True)
                    last.then_inc(a_full, 1)
                if kind == "max_rows":
                    pe.wait_ge(a_taken, a_units_until(job))
                    pe.transpose(psM[0:NT * NH, bank, 0:P], negmax[:, b, :], ident[:, :]).then_inc(misc_full[bank], 1)
                if kind == "scores_exp":
                    u, bank = st["u"], unit % 2
                    if g == 0 and u == 0:
                        pe.wait_ge(maxrow_in[b], 64 * (s + 1))
                    if unit >= 2:
                        pe.wait_ge(b_taken, unit - 1)
                    if s == 0 and u < 2:
                        heads, t, q0 = range(g * GH + 2 * u, g * GH + 2 * u + 2), 0, 0
                    elif s == 0:
                        heads, t, q0 = range(g * GH, (g + 1) * GH), 1, P
                    else:
                        heads, t, q0 = range(g * GH + 2 * (u % 2), g * GH + 2 * (u % 2) + 2), u // 2, 0
                    n = S - q0
                    for i, h in enumerate(heads):
                        last = pe.matmul(psB[:, bank, i * n:(i + 1) * n], stackK[:, b, h, t * P:(t + 1) * P],
                                         stackQ[:, b, h, q0:S], start=(s == 1 or i == 0), stop=(s == 1),
                                         skip_group_check=True)
                    if s == 0:
                        blocks = psB[:, bank].rearrange("p (h q) -> p h q", h=len(heads))[:, :, 0:P]
                        last = pe.matmul(blocks, ident16[:, :], mask16T[:, 0:len(heads), :], start=False, stop=True,
                                         skip_group_check=True)
                    last.then_inc(b_full, 1)
                if kind == "values":
                    grp, t = job * NG + g, st["u"]
                    if t == 0:
                        if grp >= 2:
                            pe.wait_ge(v_taken, grp - 1)
                        if g == 0:
                            taken("v_self" if s == 0 else "v_cross", s, b)
                        pe.wait_ge(b_taken, b_units_until(grp))
                    q0 = P if s == 0 and t == 1 else 0
                    for i in range(GH):
                        last = pe.matmul(psV[i * VW:(i + 1) * VW, grp % 2, q0:S], V[:, b, t, g * GH + i, :],
                                         E[:, grp % 3, i, t, q0:S], start=(t == 0), stop=(t == 1),
                                         skip_group_check=True, tile_position=(0, i * VW))
                    if t == 1:
                        last.then_inc(v_full, 1)
                if kind == "o_turn":
                    pe.wait_ge(v_taken, NG * (job + 1))
                    for t, (bank, k) in enumerate(misc):
                        misc_free(bank, k)
                        for i in range(NG):
                            last = pe.transpose(psM[:, bank, i * P:(i + 1) * P], oT[:, job % 2, i, t * P:(t + 1) * P],
                                                ident[:, :])
                        last.then_inc(misc_full[bank], 1)
                if kind == "o_back":
                    taken("o_turn", s, b)
                    turn(oN[:, job % 2], bank).then_inc(misc_full[bank], 1)
                if kind == "o_proj":
                    taken("o_back", s, b)
                    w = wS[:, 5, :] if s == 0 else wC[:, 3, :]
                    for t in range(NT):
                        last = pe.matmul(psM[:, bank, t * P:(t + 1) * P], oNT[:, job % 2, t * P:(t + 1) * P], w,
                                         start=True, stop=True)
                    last.then_inc(misc_full[bank], 1)
                if kind == "route":
                    if b == 0:
                        pe.wait_ge(gate_in, 16)
                    pe.wait_ge(seqrep, b + 1)
                    pe.matmul(psM[:, bank, 0:NE], xn[:, b, 0, :], gate_sb[:, :], start=True,
                              stop=True).then_inc(misc_full[bank], 1)
                if kind == "moe_up":
                    n = b * TOPK + s
                    if n == 0:
                        taken("ln_turn", 2, b)
                        pe.wait_ge(a_taken, a_total)
                        pe.wait_ge(b_taken, b_total)
                    if n >= 2:
                        pe.wait_ge(gelu_done, NC * (n - 1))
                    pe.wait_ge(w1_in[n % NW], 16 * (n // NW + 1))
                    ps = (psA, psB)[n % 2]
                    for c in range(NC):
                        last = pe.matmul(ps[:, c // 2, (c % 2) * S:(c % 2 + 1) * S],
                                         w1s[:, n % NW, c * P:(c + 1) * P], xnT[:, b, :], start=True, stop=True)
                        if c % 2:
                            last.then_inc(up_full, 1)
                if kind == "moe_down":
                    n = b * TOPK + s
                    if n == 0:
                        pe.wait_ge(v_taken, NJOB * NG)
                    if s == 0:
                        if b >= 2:
                            pe.wait_ge(y_taken, b - 1)
                        pe.wait_ge(b2_scaled, TOPK * (b + 1))
                        for t in range(NT):
                            for k in range(TOPK):
                                pe.matmul(psV[:, b % 2, t * P:(t + 1) * P], ones[0:1, :], b2row[:, b, k, :],
                                          start=(t == 0 and k == 0), stop=False, skip_group_check=True)
                    pe.wait_ge(w2_scaled, n + 1)
                    for c in range(NC):
                        pe.wait_ge(gelu_done, NC * n + c + 1)
                        for t in range(NT):
                            last = pe.matmul(psV[:, b % 2, t * P:(t + 1) * P], hid[:, n % 2, c, t * P:(t + 1) * P],
                                             w2s[:, n % NW, c, :], start=False,
                                             stop=(s == TOPK - 1 and c == NC - 1), skip_group_check=True)
                    last.then_inc(down_done, 1)


ONES16 = 1.0 + 0x3F80 * 2.0 ** -23


def kernel(x, ctx_1024, L0_attn_Wq, L0_attn_Wk, L0_attn_Wv, L0_attn_Wo, L0_xattn_W_kv, L0_xattn_W_q,
           L0_xattn_W_proj, L0_xattn_b_proj, L0_ffn_gate_w, L0_ffn_w1, L0_ffn_b1, L0_ffn_w2, L0_ffn_b2):
    import numpy as np
    import concourse.bacc as bacc
    from concourse.bass_utils import run_bass_kernel_spmd as run

    by_dim = np.arange(NH * HD).reshape(NH, HD).T.reshape(-1)
    turned = np.roll(np.arange(NH * HD).reshape(NH, HD), HD // 2, axis=1).T.reshape(-1)
    wq, wk = np.asarray(L0_attn_Wq), np.asarray(L0_attn_Wk)
    w_self = np.stack([wq[by_dim].T, wk[by_dim].T, wq[turned].T, wk[turned].T,
                       np.asarray(L0_attn_Wv).T, np.asarray(L0_attn_Wo).T], axis=1)
    kv = np.asarray(L0_xattn_W_kv)
    w_cross = np.stack([np.asarray(L0_xattn_W_q)[:, by_dim], kv[:, :D][:, by_dim], kv[:, D:],
                        np.asarray(L0_xattn_W_proj)], axis=1)
    freq = np.float32(1.0) / np.float32(10000.0) ** (np.arange(0, HD, 2, dtype=np.float32) / np.float32(HD))
    angle = np.outer(np.arange(S, dtype=np.float32), freq.astype(np.float32)).astype(np.float32)
    angle = np.concatenate([angle, angle], axis=1).T
    sign = np.where(np.arange(HD) < HD // 2, -1.0, 1.0).astype(np.float32)[:, None]
    rope = np.stack([np.repeat(np.cos(angle), NH, axis=0), np.repeat(np.sin(angle) * sign, NH, axis=0)], axis=1)

    b1_chunks = np.asarray(L0_ffn_b1).reshape(NE, NC, P).transpose(0, 2, 1)
    w1_biases = np.concatenate([np.asarray(L0_ffn_w1), b1_chunks], axis=2)
    w2_bias = np.concatenate([np.asarray(L0_ffn_w2), np.asarray(L0_ffn_b2)[:, None]], axis=1)

    arrays = {
        "x_dram": x, "ctx_dram": ctx_1024, "w_self_dram": w_self, "w_cross_dram": w_cross,
        "b_proj_dram": np.asarray(L0_xattn_b_proj), "rope_dram": rope.astype(np.float32), "gate_dram": L0_ffn_gate_w,
        "w1_dram": w1_biases, "w2_dram": w2_bias,
    }
    arrays = {k: np.ascontiguousarray(v) for k, v in arrays.items()}
    nc = bacc.Bacc("TRN2", target_bir_lowering=False, num_devices=1)
    args = [nc.dram_tensor(k, v.shape, mybir.dt.from_np(v.dtype), kind="ExternalInput").ap() for k, v in arrays.items()]
    out = nc.dram_tensor("out_dram", (NB, S, D), F32, kind="ExternalOutput").ap()
    build(nc, *args, out)
    r = run(nc, [arrays], core_ids=[0])
    return r.results[0]["out_dram"]
```

```python
from contextlib import ExitStack

import concourse.bass as bass
from concourse import mybir

ALU = mybir.AluOpType
ACT = mybir.ActivationFunctionType
AX_X = mybir.AxisListType.X
F32 = mybir.dt.float32
BF16 = mybir.dt.bfloat16
U32 = mybir.dt.uint32

NB, S, D = 4, 256, 128
P = 128
NT = S // P
NH, HD = 16, 8
NG, GH = 4, 4
NE, TOPK, FF = 8, 2, 512
NC = FF // P
NPART = 3
ROWS = 96
MAXROW = 96
VW = 32
SCALE = float(HD) ** -0.5
EPS = 1e-5
MASKED = -2.0 ** 100
LAG = 12
NJOB = 2 * NB
GRP_UNITS = (3, 4)


def plan():
    extra = {}

    def put(half, *step):
        extra.setdefault(half, []).append(step)

    start = [("ln_stats", 0, 0), ("ln_apply", 0, 0), ("ln_turn", 0, 0), ("ln_stats", 0, 1),
             ("ln_stats", 0, 2), ("ln_stats", 0, 3), ("ln_apply", 0, 1), ("init_stack", 0, 0), ("qk_self", 0, 0), ("ln_turn", 0, 1), ("constants", 0, 0), ("stack_write", 0, 0), ("stack_read", 0, 0),
             ("ln_apply", 0, 2), ("ln_apply", 0, 3), ("qk_self", 0, 1),
             ("ln_turn", 0, 2), ("ln_turn", 0, 3), ("ctx_turn", 1, 0), ("ctx_turn", 1, 1), ("ctx_turn", 1, 2),
             ("ctx_turn", 1, 3), ("init_v", 0, 0),
             ("init_stack", 0, 1), ("stack_write", 0, 1), ("stack_read", 0, 1), ("v_self", 0, 0), ("init_v", 0, 1)]
    for b in (2, 3):
        n = 8 * b - 16
        put(n + 1, "qk_self", 0, b)
        put(n + 7, "init_stack", 0, b)
        put(n + 9, "stack_write", 0, b)
        put(n + 11, "stack_read", 0, b)
        put(n + 13, "init_v", 0, b)
    for b in range(1, NB):
        put(8 * b + 1, "v_self", 0, b)
    for j in range(NJOB):
        s, b = divmod(j, NB)
        n = 2 * NG * j
        put(n + 2 * NG, "max_rows", s, b)
        m = n + LAG + 10
        put(m, "o_turn", s, b)
        put(m + 1, "o_back", s, b)
        put(m + 2, "o_proj", s, b)
        put(m + 2, "ln_stats", s + 1, b)
        put(m + 3, "ln_apply", s + 1, b)
        put(m + 4, "ln_turn", s + 1, b)
        if s == 0:
            put(m - 2, "k_cross", 1, b)
            put(m + 3, "stack_write_k", 1, b)
            put(m + 3, "v_cross", 1, b)
            put(m + 4, "stack_read_k", 1, b)
            put(m + 5, "q_cross", 1, b)
            put(m + 5, "stack_write", 1, b)
            put(m + 7, "stack_read", 1, b)
        else:
            put(m + 5, "route_mean", 2, b)
            put(m + 6, "route", 2, b)
            put(m + 7, "route_pick", 2, b)
    ffn = [("moe_up", 0), ("moe_up", 1), ("moe_down", 0)]
    for n in range(2, 2 * NB):
        ffn += [("moe_up", n), ("moe_down", n - 1)]
        if n % 2 == 0:
            ffn.append(("moe_out", n - 1))
    ffn += [("moe_down", 2 * NB - 1), ("moe_out", 2 * NB - 1)]
    last = 2 * NG * NJOB + LAG
    for half, k in ((last + 1, 3), (last + 3, 2), (last + 5, 3), (last + 7, 3)):
        for f in ffn[:k]:
            put(half, f[0], f[1] % 2, f[1] // 2)
        del ffn[:k]

    order = list(start)
    for half in range(last + 14):
        units = []
        for kind, m in (("scores_max", half), ("scores_exp", half - LAG)):
            n, h = divmod(m, 2)
            if 0 <= n < NJOB * NG:
                s, b = divmod(n // NG, NB)
                units += [(u - 2 * h, (kind, s, b, n % NG, u)) for u in range(2 * h, min(2 * h + 2, GRP_UNITS[s]))]
        order += [step for _, step in sorted(units, key=lambda unit: unit[0])]
        n, h = divmod(half - LAG - 2, 2)
        if 0 <= n < NJOB * NG:
            order.append(("values", *divmod(n // NG, NB), n % NG, h))
        order += extra.get(half, [])
    order += [(f[0], f[1] % 2, f[1] // 2) for f in ffn]

    uses = {"ln_turn": 1, "qk_self": 2, "v_self": 1, "ctx_turn": 1, "k_cross": 1, "v_cross": 1, "q_cross": 1,
            "max_rows": 1, "o_turn": 2, "o_back": 1, "o_proj": 1, "route": 1}
    count, total, steps = [0, 0], 0, []
    a_unit = b_unit = 0
    norms = {}
    for kind, s, b, *g in order:
        misc = []
        for _ in range(uses.get(kind, 0)):
            bank = total % 2
            count[bank] += 1
            misc.append((bank, count[bank]))
            total += 1
        st = dict(kind=kind, s=s, b=b, g=g[0] if g else 0, u=g[1] if g else 0, misc=misc, unit=0, norm=norms.get(kind, 0))
        if kind == "scores_max":
            st["unit"] = a_unit
            a_unit += 1
        if kind == "scores_exp":
            st["unit"] = b_unit
            b_unit += 1
        norms[kind] = norms.get(kind, 0) + 1
        steps.append(st)
    return steps, a_unit, b_unit


def a_units_until(job):
    return sum(NG * GRP_UNITS[j // NB] for j in range(job + 1))


def b_units_until(group):
    return sum(GRP_UNITS[n // (NG * NB)] for n in range(group + 1))


def build(nc, x, ctx_in, w_self, w_cross, b_proj, rope, gate_w, w1_biases, w2, out):
    steps, a_total, b_total = plan()
    use = {(st["kind"], st["s"], st["b"]): st["misc"] for st in steps if st["misc"]}

    scratch = nc.dram_tensor("scratch", [2, NB, 2, NPART, P, S], BF16).ap()

    with ExitStack() as ctx:
        def sb(name, shape, dt=F32):
            return ctx.enter_context(nc.sbuf_tensor(name, shape, dt))

        def sem(name):
            return ctx.enter_context(nc.semaphore(name))

        def sems(name, n=NB):
            return [sem(f"{name}{i}") for i in range(n)]

        res = sb("res", [P, NB, NT, D])
        ctx_tok = sb("ctx_tok", [P, NB, NT, D])
        wS = sb("wS", [P, 6, D])
        wC = sb("wC", [P, 4, D])
        gate_sb = sb("gate_sb", [P, NE])
        rope_sb = sb("rope_sb", [P, 2, S])
        bproj = sb("bproj", [P, D])
        ident = sb("ident", [P, P])
        ident16 = sb("ident16", [P, P], BF16)
        mask16 = sb("mask16", [P, GH, P], BF16)
        mask16T = sb("mask16T", [P, GH, P], BF16)
        ones = sb("ones", [P, P])
        neg_half = sb("neg_half", [P, NT])
        euler = sb("euler", [P, NE])
        stats = sb("stats", [P, NB, NT, 6])
        mv = sb("mv", [P, NB, NT, 2])
        rstd = sb("rstd", [P, NB, NT])
        xn = sb("xn", [P, NB, NT, D])
        xnT = sb("xnT", [P, NB, S])
        ctxT = sb("ctxT", [P, NB, S])
        rot = sb("rot", [P, 2, 2, 2, S])
        kc = sb("kc", [P, 2, S])
        parts = sb("parts", [P, NB, 2, NPART, S], BF16)
        stackQ = sb("stackQ", [MAXROW + 2, NB, NH, S], BF16)
        stackK = sb("stackK", [MAXROW + 2, NB, NH, S], BF16)
        V = sb("V", [P, NB, NT, NH, VW])
        negmax = sb("negmax", [P, NB, NH, NT])
        maxT = sb("maxT", [NT * NH, NB, 2, P], BF16)
        E = sb("E", [P, 3, GH, NT, S])
        oT = sb("oT", [P, 2, NG, S])
        rden = sb("rden", [P, 2, NT, NH])
        oN = sb("oN", [P, 2, NT, D])
        oNT = sb("oNT", [P, 2, S])
        seqsum = sb("seqsum", [P, NB, 1])
        small = sb("small", [P, NB, 8, NE])
        top_i = sb("top_i", [P, NB, NE], U32)
        b2row = sb("b2row", [1, NB, TOPK, D])
        NW = 4
        w1s = sb("w1s", [P, NW, FF + NC])
        w2s = sb("w2s", [P, NW, NC, D])
        hid = sb("hid", [P, 2, NC, S])

        psA = ctx.enter_context(nc.psum_tensor("psA", [P, 2, 512], F32))
        psB = ctx.enter_context(nc.psum_tensor("psB", [P, 2, 512], F32))
        psV = ctx.enter_context(nc.psum_tensor("psV", [P, 2, 512], F32))
        psM = ctx.enter_context(nc.psum_tensor("psM", [P, 2, 512], F32))

        x_in, ctx_loaded = sems("x_in"), sem("ctx_loaded")
        wS_in, wC_in, rope_in = sem("wS_in"), sem("wC_in"), sem("rope_in")
        gate_in, bproj_in = sem("gate_in"), sem("bproj_in")
        ones_set, ident_set, consts, stack_init, v_init = sem("ones_set"), sem("ident_set"), sem("consts"), sems("stack_init"), sem("v_init")
        misc_full, misc_taken = sems("misc_full", 2), sems("misc_taken", 2)
        var_ready, rstd_ready, xn_ready = sem("var_ready"), sem("rstd_ready"), sem("xn_ready")
        parts_self, parts_k, parts_q = sems("parts_self"), sems("parts_k"), sems("parts_q")
        scr_q, scr_k, part_written = sems("scr_q"), sems("scr_k"), sems("part_written", NB * NPART)
        q_in, k_in, maxrow_in = sems("q_in"), sems("k_in"), sems("maxrow_in")
        a_full, a_taken = sem("a_full"), sem("a_taken")
        b_full, b_taken = sem("b_full"), sem("b_taken")
        v_full, v_taken = sem("v_full"), sem("v_taken")
        oN_ready = sem("oN_ready")
        probs_ready = sem("probs_ready")
        seqrep, bias_added = sem("seqrep"), sem("bias_added")
        chosen, weights_ready = sem("chosen"), sem("weights_ready")
        b2_in, b2_scaled = sems("b2_in"), sem("b2_scaled")
        w1_in, w2_in, w2_scaled = sems("w1_in", NW), sems("w2_in", NW), sem("w2_scaled")
        up_full, gelu_done, down_done = sem("up_full"), sem("gelu_done"), sem("down_done")
        y_taken = sem("y_taken")
        stored = sem("stored")
        dve_own, pool_own, act_own = sem("dve_own"), sem("pool_own"), sem("act_own")

        block = ctx.enter_context(nc.Block())

        @block.sync
        def _(sp):
            for b in range(NB):
                sp.dma_start(res[:, b], x[b].rearrange("(t p) d -> p t d", p=P)).then_inc(x_in[b], 16)
                if b == 0:
                    sp.dma_start(wS[:, :, :], w_self).then_inc(wS_in, 16)
                    sp.dma_start(rope_sb[:, :, :], rope).then_inc(rope_in, 16)
            sp.dma_start(ctx_tok[:, :, :, :],
                         ctx_in.rearrange("b (t p) d -> p (b t) d", p=P)).then_inc(ctx_loaded, 16)
            sp.dma_start(wC[:, :, :], w_cross).then_inc(wC_in, 16)
            sp.dma_start(gate_sb[:, :], gate_w).then_inc(gate_in, 16)
            sp.dma_start(bproj[:, :], b_proj.partition_broadcast(P)).then_inc(bproj_in, 16)

            def write_parts(s, b, which, done):
                sp.dma_start(scratch[s, b, which].rearrange("i p t -> p i t"), parts[:, b, which]).then_inc(done, 16)

            def write_both(b, i):
                sp.dma_start(scratch[0, b, :, i].rearrange("w p t -> p w t"), parts[:, b, :, i]).then_inc(part_written[b * NPART + i], 16)

            def read_q(s, b, i):
                r = i * NPART * HD
                src = scratch[s, b, 0, i]
                thrice = bass.AP(src.tensor, src.offset, [[0, NPART], [NH * S, HD], [1, NH * S]])
                sp.dma_start(stackQ[r:r + NPART * HD, b], thrice).then_inc(q_in[b], 16)

            def read_k(s, b):
                for i in range(NPART):
                    r = i * NPART * HD
                    sp.dma_start(stackK[r:r + NPART * HD, b],
                                 scratch[s, b, 1].rearrange("i (d h) t -> (i d) h t", h=NH)).then_inc(k_in[b], 16)

            for st in steps:
                kind, s, b = st["kind"], st["s"], st["b"]
                if kind == "stack_write" and s == 0:
                    for i in range(NPART):
                        sp.wait_ge(parts_self[b], i + 1)
                        write_both(b, i)
                if kind == "stack_read" and s == 0:
                    sp.wait_ge(stack_init[b], 2)
                    for i in range(NPART - 1):
                        sp.wait_ge(part_written[b * NPART + i], 16)
                        read_q(s, b, i)
                    sp.wait_ge(part_written[b * NPART + NPART - 1], 16)
                    read_k(s, b)
                    read_q(s, b, NPART - 1)
                if kind == "stack_write_k":
                    sp.wait_ge(parts_k[b], NPART)
                    write_parts(s, b, 1, scr_k[b])
                if kind == "stack_read_k":
                    sp.wait_ge(b_full, b_units_until(NG * (b + 1) - 1))
                    sp.wait_ge(scr_k[b], 16)
                    read_k(s, b)
                if kind == "stack_write" and s == 1:
                    sp.wait_ge(parts_q[b], 1)
                    write_parts(s, b, 0, scr_q[b])
                if kind == "stack_read" and s == 1:
                    sp.wait_ge(scr_q[b], 16)
                    for i in range(NPART):
                        read_q(s, b, i)
                if kind == "max_rows":
                    sp.wait_ge(misc_taken[st["misc"][0][0]], st["misc"][0][1])
                    for i in range(2):
                        sp.dma_start(stackQ[MAXROW + i:MAXROW + i + 1, b].rearrange("o h (t q) -> o (h t) q", t=NT),
                                     maxT[:, b, i, :]).then_inc(maxrow_in[b], 16)
                if kind == "route_pick":
                    sp.wait_ge(chosen, b + 1)
                    for k in range(TOPK):
                        n = b * TOPK + k
                        e = sp.value_load(top_i[0:1, b, k:k + 1], min_val=0, max_val=NE - 1)
                        if n >= NW:
                            sp.wait_ge(down_done, n - NW + 1)
                        sp.dma_start(w1s[:, n % NW, :],
                                     w1_biases[bass.ds(e, 1), 0:P].rearrange("e p f -> p (e f)")).then_inc(w1_in[n % NW], 16)
                        sp.dma_start(w2s[:, n % NW, :, :],
                                     w2[bass.ds(e, 1), 0:FF].rearrange("e (c p) d -> p (e c) d", p=P)).then_inc(w2_in[n % NW], 16)
                        sp.dma_start(b2row[:, b, k, :],
                                     w2[bass.ds(e, 1), FF:FF + 1].rearrange("e o d -> (e o) d")).then_inc(b2_in[b], 16)
                if kind == "moe_out":
                    sp.wait_ge(y_taken, b + 1)
                    sp.dma_start(out[b].rearrange("(t p) d -> p t d", p=P), res[:, b]).then_inc(stored, 16)
            sp.wait_ge(stored, 16 * NB)

        @block.gpsimd
        def _(pool):
            own = [0]

            def then(ins):
                own[0] += 1
                ins.then_inc(pool_own, 1)
                pool.wait_ge(pool_own, own[0])

            def split(src, dst, ready):
                pool.tensor_copy(dst[:, :, 0], src).then_inc(ready, 1)
                pool.wait_ge(ready, 1)
                then(pool.tensor_tensor(src, src, dst[:, :, 0], ALU.subtract))
                pool.tensor_copy(dst[:, :, 1], src).then_inc(ready, 1)
                pool.wait_ge(ready, 2)
                pool.tensor_tensor(dst[:, :, 2], src, dst[:, :, 1], ALU.subtract).then_inc(ready, 1)

            def constants():
                pool.memset(euler[:, :], 2.718281828459045).then_inc(consts, 1)
                then(pool.memset(ident16[:, :], 0.0))
                pool.affine_select(out=ident16[:, :], in_=ident16[:, :], compare_op=ALU.not_equal, fill=1.0, base=0,
                                   pattern=[[-1, P]], channel_multiplier=1).then_inc(consts, 1)
                for m, sign in ((mask16, 1), (mask16T, -1)):
                    then(pool.memset(m[:, :, :], 0.0))
                    pool.affine_select(out=m[:, :, :], in_=m[:, :, :], compare_op=ALU.is_ge, fill=MASKED, base=0,
                                       pattern=[[0, GH], [-sign, P]], channel_multiplier=sign).then_inc(consts, 1)

            pool.memset(ones[:, :], 1.0).then_inc(ones_set, 1)
            then(pool.memset(neg_half[:, :], -0.5))
            then(pool.memset(ident[:, :], 0.0))
            pool.affine_select(out=ident[:, :], in_=ident[:, :], compare_op=ALU.not_equal, fill=1.0, base=0,
                               pattern=[[-1, P]], channel_multiplier=1).then_inc(ident_set, 1)

            def init_v(b):
                then(pool.memset(V[:, b], 0.0))
                pool.memset(V[:, b, :, :, HD:HD + 1], 1.0).then_inc(v_init, 1)
                pool.wait_ge(v_init, b + 1)

            def init_stack(b):
                pool.memset(stackQ[0:ROWS, b].bitcast(F32), 0.0).then_inc(stack_init[b], 1)
                pool.memset(stackK[:, b].bitcast(F32), ONES16).then_inc(stack_init[b], 1)

            def rsqrt_var(n, b):
                pool.wait_ge(var_ready, n + 1)
                then(pool.tensor_scalar(rstd[:, b, :], mv[:, b, :, 1], EPS, None, ALU.add))
                pool.tensor_tensor(rstd[:, b, :], rstd[:, b, :], neg_half[:, :], ALU.pow).then_inc(rstd_ready, 1)
                pool.wait_ge(rstd_ready, n + 1)

            for st in steps:
                kind, s, b, misc, unit = st["kind"], st["s"], st["b"], st["misc"], st["unit"]
                if kind == "ln_stats":
                    rsqrt_var(st["norm"], b)
                if kind == "constants":
                    constants()
                if kind == "init_v":
                    init_v(b)
                if kind == "init_stack":
                    init_stack(b)
                if kind == "qk_self" and b >= 2:
                    for bank, k in misc:
                        pool.wait_ge(misc_taken[bank], k)
                    cs, sn = rot[:, b % 2, 0], rot[:, b % 2, 1]
                    then(pool.tensor_tensor(cs, cs, sn, ALU.add))
                    split(cs, parts[:, b], parts_self[b])
                if kind == "q_cross":
                    if b == 0:
                        pool.wait_ge(bproj_in, 16)
                    pool.wait_ge(xn_ready, NB + b + 1)
                    pool.tensor_tensor(res[:, b], res[:, b],
                                       bproj[:, :].rearrange("p (o d) -> p o d", o=1).to_broadcast([P, NT, D]),
                                       ALU.add).then_inc(bias_added, 1)
                if kind == "k_cross":
                    bank, k = misc[0]
                    pool.wait_ge(misc_taken[bank], k)
                    kk = kc[:, b % 2:b % 2 + 1]
                    split(kk, parts[:, b, 1:2], parts_k[b])
                if kind == "route":
                    bank, k = misc[0]
                    pool.wait_ge(misc_taken[bank], k)
                    pool.tensor_tensor(small[:, b, 1], euler[:, :], small[:, b, 0], ALU.pow).then_inc(probs_ready, 1)
                if kind == "moe_up" and s == 0:
                    pool.wait_ge(weights_ready, b + 1)
                    pool.wait_ge(b2_in[b], 16 * TOPK)
                    for k in range(TOPK):
                        pool.tensor_scalar(b2row[:, b, k], b2row[:, b, k], small[0:1, b, 6, k:k + 1], None,
                                           ALU.mult).then_inc(b2_scaled, 1)

        @block.vector
        def _(dve):
            own = [0]

            def then(ins):
                own[0] += 1
                ins.then_inc(dve_own, 1)
                dve.wait_ge(dve_own, own[0])

            def split(src, dst, ready):
                dve.tensor_copy(dst[:, :, 0], src).then_inc(ready, 1)
                dve.wait_ge(ready, 1)
                then(dve.tensor_tensor(src, src, dst[:, :, 0], ALU.subtract))
                dve.tensor_copy(dst[:, :, 1], src).then_inc(ready, 1)
                dve.wait_ge(ready, 2)
                dve.tensor_tensor(dst[:, :, 2], src, dst[:, :, 1], ALU.subtract).then_inc(ready, 1)

            for st in steps:
                kind, s, b, g, misc, unit = st["kind"], st["s"], st["b"], st["g"], st["misc"], st["unit"]
                job = s * NB + b
                if kind == "ln_stats":
                    if s == 0:
                        dve.wait_ge(x_in[b], 16)
                    for t in range(NT):
                        last = dve.bn_stats(stats[:, b, t, :], res[:, b, t, :])
                        if t == NT - 1:
                            then(last)
                    for t in range(NT):
                        last = dve.bn_aggr(mv[:, b, t, :], stats[:, b, t, :])
                    last.then_inc(var_ready, 1)
                if kind == "ln_apply":
                    dve.wait_ge(rstd_ready, st["norm"] + 1)
                    for t in range(NT):
                        last = dve.tensor_scalar(xn[:, b, t, :], res[:, b, t, :], mv[:, b, t, 0:1], rstd[:, b, t:t + 1],
                                                 ALU.subtract, ALU.mult)
                    last.then_inc(xn_ready, 1)
                if kind == "qk_self":
                    if b == 0:
                        dve.wait_ge(rope_in, 16)
                    for i, (bank, k) in enumerate(misc):
                        dve.wait_ge(misc_full[bank], k)
                        table = rope_sb[:, i:i + 1, :].to_broadcast([P, 2, S])
                        dve.tensor_tensor(rot[:, b % 2, i], psM[:, bank].rearrange("p (a t) -> p a t", a=2), table,
                                          ALU.mult).then_inc(misc_taken[bank], 1)
                    if b < 2:
                        for bank, k in misc:
                            dve.wait_ge(misc_taken[bank], k)
                        cs = rot[:, b % 2, 0]
                        then(dve.tensor_tensor(cs, cs, rot[:, b % 2, 1], ALU.add))
                        split(cs, parts[:, b], parts_self[b])
                if kind == "q_cross":
                    bank, k = misc[0]
                    dve.wait_ge(misc_full[bank], k)
                    qq, dst = rot[:, b % 2, 0, 0], parts[:, b, 0]
                    then(dve.tensor_copy(dst[:, 0], psM[:, bank, 0:S]))
                    dve.tensor_tensor(qq, psM[:, bank, 0:S], dst[:, 0], ALU.subtract).then_inc(misc_taken[bank], 1)
                    dve.wait_ge(misc_taken[bank], k)
                    then(dve.tensor_copy(dst[:, 1], qq))
                    dve.tensor_tensor(dst[:, 2], qq, dst[:, 1], ALU.subtract).then_inc(parts_q[b], 1)
                if kind == "scores_max":
                    u, bank = st["u"], unit % 2
                    dve.wait_ge(a_full, unit + 1)
                    if s == 0 and u == 0:
                        h, nh, t = g * GH, GH, 0
                    elif s == 0:
                        h, nh, t = g * GH + 2 * (u - 1), 2, 1
                    else:
                        h, nh, t = g * GH + 2 * (u % 2), 2, u // 2
                    dve.tensor_reduce(negmax[:, b, h:h + nh, t], psA[:, bank].rearrange("p (h k) -> p h k", h=nh),
                                      AX_X, ALU.max, negate=True).then_inc(a_taken, 1)
                if kind == "max_rows":
                    bank, k = misc[0]
                    dve.wait_ge(misc_full[bank], k)
                    if s == 1:
                        dve.wait_ge(maxrow_in[b], 32)
                    m = psM[0:NT * NH, bank, 0:P]
                    then(dve.tensor_copy(maxT[:, b, 0, :], m))
                    dve.tensor_tensor(maxT[:, b, 1, :], m, maxT[:, b, 0, :], ALU.subtract).then_inc(misc_taken[bank], 1)
                if kind == "o_turn":
                    for t, (bank, k) in enumerate(misc):
                        dve.wait_ge(misc_full[bank], k)
                        o = psM[:, bank].rearrange("p (h c) -> p h c", c=VW)
                        then(dve.reciprocal(rden[:, job % 2, t, :], o[:, :, HD]))
                        r = rden[:, job % 2, t, :].rearrange("p (h o) -> p h o", o=1).to_broadcast([P, NH, HD])
                        dve.tensor_tensor(oN[:, job % 2, t, :].rearrange("p (h c) -> p h c", c=HD), o[:, :, 0:HD], r,
                                          ALU.mult).then_inc(misc_taken[bank], 1)
                if kind == "o_proj":
                    bank, k = misc[0]
                    dve.wait_ge(misc_full[bank], k)
                    if s == 1:
                        dve.wait_ge(bias_added, b + 1)
                    y = psM[:, bank, 0:S].rearrange("p (t d) -> p t d", t=NT)
                    dve.tensor_tensor(res[:, b], res[:, b], y, ALU.add).then_inc(misc_taken[bank], 1)
                    dve.wait_ge(misc_taken[bank], k)
                if kind == "route_mean":
                    turned = use[("ln_turn", 2, b)][0]
                    dve.wait_ge(misc_taken[turned[0]], turned[1])
                    dve.tensor_scalar(xn[:, b, 0, :], ones[:, :], seqsum[:, b, 0:1], 1.0 / S, ALU.mult,
                                      ALU.mult).then_inc(seqrep, 1)
                if kind == "route":
                    bank, k = misc[0]
                    dve.wait_ge(misc_full[bank], k)
                    v = small[:, b]
                    then(dve.tensor_reduce(v[:, 3, 0:1], psM[:, bank, 0:NE], AX_X, ALU.max))
                    dve.tensor_scalar(v[:, 0], psM[:, bank, 0:NE], v[:, 3, 0:1], None,
                                      ALU.subtract).then_inc(misc_taken[bank], 1)
                if kind == "route_pick":
                    v = small[:, b]
                    dve.wait_ge(probs_ready, b + 1)
                    then(dve.max(v[:, 4], v[:, 1]))
                    dve.max_index(top_i[:, b, :], v[:, 4], v[:, 1]).then_inc(chosen, 1)
                    then(dve.tensor_tensor(v[:, 5, 0:1], v[:, 4, 0:1], v[:, 4, 1:2], ALU.add))
                    then(dve.reciprocal(v[:, 5, 1:2], v[:, 5, 0:1]))
                    dve.tensor_scalar(v[:, 6, 0:TOPK], v[:, 4, 0:TOPK], v[:, 5, 1:2], None,
                                      ALU.mult).then_inc(weights_ready, 1)
                    dve.wait_ge(weights_ready, b + 1)
                if kind == "moe_up":
                    n = b * TOPK + s
                    dve.wait_ge(w2_in[n % NW], 16 * (n // NW + 1))
                    dve.tensor_scalar(w2s[:, n % NW], w2s[:, n % NW], small[:, b, 6, s:s + 1], None,
                                      ALU.mult).then_inc(w2_scaled, 1)
                if kind == "moe_out":
                    dve.wait_ge(down_done, TOPK * (b + 1))
                    dve.tensor_tensor(res[:, b], res[:, b], psV[:, b % 2, 0:S].rearrange("p (t d) -> p t d", t=NT),
                                      ALU.add).then_inc(y_taken, 1)

        @block.scalar
        def _(act):
            for st in steps:
                kind, s, b, g, misc, unit = st["kind"], st["s"], st["b"], st["g"], st["misc"], st["unit"]
                job = s * NB + b
                if kind == "ln_turn":
                    bank, k = misc[0]
                    act.wait_ge(misc_full[bank], k)
                    if s < 2:
                        act.activation(xnT[:, b, :], psM[:, bank, 0:S], ACT.Copy).then_inc(misc_taken[bank], 1)
                    else:
                        act.activation(xnT[:, b, :], psM[:, bank, 0:S], ACT.Copy,
                                       accum_out=seqsum[:, b, 0:1]).then_inc(misc_taken[bank], 1)
                if kind == "ctx_turn":
                    bank, k = misc[0]
                    act.wait_ge(misc_full[bank], k)
                    act.activation(ctxT[:, b, :], psM[:, bank, 0:S], ACT.Copy).then_inc(misc_taken[bank], 1)
                if kind in ("v_self", "v_cross"):
                    bank, k = misc[0]
                    act.wait_ge(misc_full[bank], k)
                    if kind == "v_self":
                        act.wait_ge(v_init, b + 1)
                    else:
                        act.wait_ge(v_full, NG * (b + 1))
                    act.activation(V[:, b, :, :, 0:HD],
                                   psM[:, bank, 0:S].rearrange("p (t h d) -> p t h d", t=NT, h=NH),
                                   ACT.Copy).then_inc(misc_taken[bank], 1)
                if kind == "k_cross":
                    bank, k = misc[0]
                    act.wait_ge(misc_full[bank], k)
                    if b >= 2:
                        act.wait_ge(parts_k[b - 2], NPART)
                    act.activation(kc[:, b % 2], psM[:, bank, 0:S], ACT.Copy).then_inc(misc_taken[bank], 1)
                if kind == "scores_exp":
                    grp = job * NG + g
                    u, bank = st["u"], unit % 2
                    if grp >= 3 and u == 0:
                        act.wait_ge(v_full, grp - 2)
                    act.wait_ge(b_full, unit + 1)
                    if s == 0 and u < 2:
                        dst = E[:, grp % 3, 2 * u:2 * u + 2, 0, :]
                    elif s == 0:
                        dst = E[:, grp % 3, :, 1, P:S]
                    else:
                        dst = E[:, grp % 3, 2 * (u % 2):2 * (u % 2) + 2, u // 2, :]
                    act.activation(dst, psB[:, bank].rearrange("p (h q) -> p h q", h=dst.shape[1]), ACT.Exp,
                                   scale=SCALE).then_inc(b_taken, 1)
                if kind == "values" and st["u"] == 1:
                    grp = job * NG + g
                    act.wait_ge(v_full, grp + 1)
                    if g == 0 and job >= 2:
                        for bank, k in use[("o_turn", *divmod(job - 2, NB))]:
                            act.wait_ge(misc_full[bank], k)
                    act.activation(oT[:, job % 2, g, :], psV[:, grp % 2, 0:S], ACT.Copy).then_inc(v_taken, 1)
                if kind == "o_back":
                    bank, k = misc[0]
                    act.wait_ge(misc_full[bank], k)
                    act.activation(oNT[:, job % 2, :], psM[:, bank, 0:S], ACT.Copy).then_inc(misc_taken[bank], 1)
                if kind == "moe_up":
                    n = b * TOPK + s
                    if n >= 2:
                        act.wait_ge(down_done, n - 1)
                    ps = (psA, psB)[n % 2]
                    act.wait_ge(w1_in[n % NW], 16 * (n // NW + 1))
                    for c in range(NC):
                        if c % 2 == 0:
                            act.wait_ge(up_full, 2 * n + c // 2 + 1)
                        act.activation(hid[:, n % 2, c, :], ps[:, c // 2, (c % 2) * S:(c % 2 + 1) * S], ACT.Gelu,
                                       bias=w1s[:, n % NW, FF + c:FF + c + 1]).then_inc(gelu_done, 1)

        @block.tensor
        def _(pe):
            def misc_free(bank, k):
                if k > 1:
                    pe.wait_ge(misc_taken[bank], k - 1)

            def taken(kind, s, b):
                for bank, k in use[(kind, s, b)]:
                    pe.wait_ge(misc_taken[bank], k)

            def turn(src, bank):
                for t in range(NT):
                    last = pe.transpose(psM[:, bank, t * P:(t + 1) * P], src[:, t, :], ident[:, :])
                return last

            for st in steps:
                kind, s, b, g, misc, unit = st["kind"], st["s"], st["b"], st["g"], st["misc"], st["unit"]
                job = s * NB + b
                for bank, k in misc[:1]:
                    misc_free(bank, k)
                bank, k = misc[0] if misc else (0, 0)
                if kind == "ln_turn":
                    if s == 0 and b == 0:
                        pe.wait_ge(ident_set, 1)
                    pe.wait_ge(xn_ready, st["norm"] + 1)
                    turn(xn[:, b], bank).then_inc(misc_full[bank], 1)
                if kind == "qk_self":
                    if b == 0:
                        pe.wait_ge(wS_in, 16)
                    taken("ln_turn", 0, b)
                    for i, (bank, k) in enumerate(misc):
                        misc_free(bank, k)
                        for a in range(2):
                            last = pe.matmul(psM[:, bank, a * S:(a + 1) * S], wS[:, 2 * i + a, :], xnT[:, b, :],
                                             start=True, stop=True)
                        last.then_inc(misc_full[bank], 1)
                if kind == "v_self":
                    for t in range(NT):
                        last = pe.matmul(psM[:, bank, t * P:(t + 1) * P], xnT[:, b, t * P:(t + 1) * P], wS[:, 4, :],
                                         start=True, stop=True)
                    last.then_inc(misc_full[bank], 1)
                if kind == "ctx_turn":
                    if b == 0:
                        pe.wait_ge(ctx_loaded, 16)
                    turn(ctx_tok[:, b], bank).then_inc(misc_full[bank], 1)
                if kind == "k_cross":
                    if b == 0:
                        pe.wait_ge(wC_in, 16)
                    taken("ctx_turn", 1, b)
                    pe.matmul(psM[:, bank, 0:S], wC[:, 1, :], ctxT[:, b, :], start=True,
                              stop=True).then_inc(misc_full[bank], 1)
                if kind == "v_cross":
                    for t in range(NT):
                        last = pe.matmul(psM[:, bank, t * P:(t + 1) * P], ctxT[:, b, t * P:(t + 1) * P], wC[:, 2, :],
                                         start=True, stop=True)
                    last.then_inc(misc_full[bank], 1)
                if kind == "q_cross":
                    taken("ln_turn", 1, b)
                    pe.matmul(psM[:, bank, 0:S], wC[:, 0, :], xnT[:, b, :], start=True,
                              stop=True).then_inc(misc_full[bank], 1)
                if kind == "scores_max":
                    u, bank = st["u"], unit % 2
                    if unit == 0:
                        pe.wait_ge(consts, 4)
                    if g == 0 and u == 0:
                        pe.wait_ge(q_in[b], 16 * NPART * (s + 1))
                        pe.wait_ge(k_in[b], 16 * NPART * (s + 1))
                    if unit >= 2:
                        pe.wait_ge(a_taken, unit - 1)
                    if s == 0 and u == 0:
                        heads, t, keys = range(g * GH, (g + 1) * GH), 0, P
                    elif s == 0:
                        heads, t, keys = range(g * GH + 2 * (u - 1), g * GH + 2 * u), 1, S
                    else:
                        heads, t, keys = range(g * GH + 2 * (u % 2), g * GH + 2 * (u % 2) + 2), u // 2, S
                    for i, h in enumerate(heads):
                        last = pe.matmul(psA[:, bank, i * keys:(i + 1) * keys], stackQ[0:ROWS, b, h, t * P:(t + 1) * P],
                                         stackK[0:ROWS, b, h, 0:keys], start=(s == 1 or i == 0), stop=(s == 1),
                                         skip_group_check=True)
                    if s == 0:
                        blocks = psA[:, bank].rearrange("p (h k) -> p h k", h=len(heads))[:, :, keys - P:keys]
                        last = pe.matmul(blocks, ident16[:, :], mask16[:, 0:len(heads), :], start=False, stop=True,
                                         skip_group_check=True)
                    last.then_inc(a_full, 1)
                if kind == "max_rows":
                    pe.wait_ge(a_taken, a_units_until(job))
                    pe.transpose(psM[0:NT * NH, bank, 0:P], negmax[:, b], ident[:, :]).then_inc(misc_full[bank], 1)
                if kind == "scores_exp":
                    u, bank = st["u"], unit % 2
                    if g == 0 and u == 0:
                        pe.wait_ge(maxrow_in[b], 32 * (s + 1))
                    if unit >= 2:
                        pe.wait_ge(b_taken, unit - 1)
                    if s == 0 and u < 2:
                        heads, t, q0 = range(g * GH + 2 * u, g * GH + 2 * u + 2), 0, 0
                    elif s == 0:
                        heads, t, q0 = range(g * GH, (g + 1) * GH), 1, P
                    else:
                        heads, t, q0 = range(g * GH + 2 * (u % 2), g * GH + 2 * (u % 2) + 2), u // 2, 0
                    n = S - q0
                    for i, h in enumerate(heads):
                        last = pe.matmul(psB[:, bank, i * n:(i + 1) * n], stackK[:, b, h, t * P:(t + 1) * P],
                                         stackQ[:, b, h, q0:S], start=(s == 1 or i == 0), stop=(s == 1),
                                         skip_group_check=True)
                    if s == 0:
                        blocks = psB[:, bank].rearrange("p (h q) -> p h q", h=len(heads))[:, :, 0:P]
                        last = pe.matmul(blocks, ident16[:, :], mask16T[:, 0:len(heads), :], start=False, stop=True,
                                         skip_group_check=True)
                    last.then_inc(b_full, 1)
                if kind == "values":
                    grp, t = job * NG + g, st["u"]
                    if t == 0:
                        if grp >= 2:
                            pe.wait_ge(v_taken, grp - 1)
                        if g == 0:
                            taken("v_self" if s == 0 else "v_cross", s, b)
                        pe.wait_ge(b_taken, b_units_until(grp))
                    q0 = P if s == 0 and t == 1 else 0
                    for i in range(GH):
                        last = pe.matmul(psV[i * VW:(i + 1) * VW, grp % 2, q0:S], V[:, b, t, g * GH + i, :],
                                         E[:, grp % 3, i, t, q0:S], start=(t == 0), stop=(t == 1),
                                         skip_group_check=True, tile_position=(0, i * VW))
                    if t == 1:
                        last.then_inc(v_full, 1)
                if kind == "o_turn":
                    pe.wait_ge(v_taken, NG * (job + 1))
                    for t, (bank, k) in enumerate(misc):
                        misc_free(bank, k)
                        for i in range(NG):
                            last = pe.transpose(psM[:, bank, i * P:(i + 1) * P], oT[:, job % 2, i, t * P:(t + 1) * P],
                                                ident[:, :])
                        last.then_inc(misc_full[bank], 1)
                if kind == "o_back":
                    taken("o_turn", s, b)
                    turn(oN[:, job % 2], bank).then_inc(misc_full[bank], 1)
                if kind == "o_proj":
                    taken("o_back", s, b)
                    w = wS[:, 5, :] if s == 0 else wC[:, 3, :]
                    for t in range(NT):
                        last = pe.matmul(psM[:, bank, t * P:(t + 1) * P], oNT[:, job % 2, t * P:(t + 1) * P], w,
                                         start=True, stop=True)
                    last.then_inc(misc_full[bank], 1)
                if kind == "route":
                    if b == 0:
                        pe.wait_ge(gate_in, 16)
                    pe.wait_ge(seqrep, b + 1)
                    pe.matmul(psM[:, bank, 0:NE], xn[:, b, 0, :], gate_sb[:, :], start=True,
                              stop=True).then_inc(misc_full[bank], 1)
                if kind == "moe_up":
                    n = b * TOPK + s
                    if n == 0:
                        taken("ln_turn", 2, b)
                        pe.wait_ge(a_taken, a_total)
                        pe.wait_ge(b_taken, b_total)
                    if n >= 2:
                        pe.wait_ge(gelu_done, NC * (n - 1))
                    pe.wait_ge(w1_in[n % NW], 16 * (n // NW + 1))
                    ps = (psA, psB)[n % 2]
                    for c in range(NC):
                        last = pe.matmul(ps[:, c // 2, (c % 2) * S:(c % 2 + 1) * S],
                                         w1s[:, n % NW, c * P:(c + 1) * P], xnT[:, b, :], start=True, stop=True)
                        if c % 2:
                            last.then_inc(up_full, 1)
                if kind == "moe_down":
                    n = b * TOPK + s
                    if n == 0:
                        pe.wait_ge(v_taken, NJOB * NG)
                    if s == 0:
                        if b >= 2:
                            pe.wait_ge(y_taken, b - 1)
                        pe.wait_ge(b2_scaled, TOPK * (b + 1))
                        for t in range(NT):
                            for k in range(TOPK):
                                pe.matmul(psV[:, b % 2, t * P:(t + 1) * P], ones[0:1, :], b2row[:, b, k, :],
                                          start=(t == 0 and k == 0), stop=False, skip_group_check=True)
                    pe.wait_ge(w2_scaled, n + 1)
                    for c in range(NC):
                        pe.wait_ge(gelu_done, NC * n + c + 1)
                        for t in range(NT):
                            last = pe.matmul(psV[:, b % 2, t * P:(t + 1) * P], hid[:, n % 2, c, t * P:(t + 1) * P],
                                             w2s[:, n % NW, c, :], start=False,
                                             stop=(s == TOPK - 1 and c == NC - 1), skip_group_check=True)
                    last.then_inc(down_done, 1)


ONES16 = 1.0 + 0x3F80 * 2.0 ** -23


def kernel(x, ctx_1024, L0_attn_Wq, L0_attn_Wk, L0_attn_Wv, L0_attn_Wo, L0_xattn_W_kv, L0_xattn_W_q,
           L0_xattn_W_proj, L0_xattn_b_proj, L0_ffn_gate_w, L0_ffn_w1, L0_ffn_b1, L0_ffn_w2, L0_ffn_b2):
    import numpy as np
    import concourse.bacc as bacc
    from concourse.bass_utils import run_bass_kernel_spmd as run

    by_dim = np.arange(NH * HD).reshape(NH, HD).T.reshape(-1)
    turned = np.roll(np.arange(NH * HD).reshape(NH, HD), HD // 2, axis=1).T.reshape(-1)
    wq, wk = np.asarray(L0_attn_Wq), np.asarray(L0_attn_Wk)
    w_self = np.stack([wq[by_dim].T, wk[by_dim].T, wq[turned].T, wk[turned].T,
                       np.asarray(L0_attn_Wv).T, np.asarray(L0_attn_Wo).T], axis=1)
    kv = np.asarray(L0_xattn_W_kv)
    w_cross = np.stack([np.asarray(L0_xattn_W_q)[:, by_dim], kv[:, :D][:, by_dim], kv[:, D:],
                        np.asarray(L0_xattn_W_proj)], axis=1)
    freq = np.float32(1.0) / np.float32(10000.0) ** (np.arange(0, HD, 2, dtype=np.float32) / np.float32(HD))
    angle = np.outer(np.arange(S, dtype=np.float32), freq.astype(np.float32)).astype(np.float32)
    angle = np.concatenate([angle, angle], axis=1).T
    sign = np.where(np.arange(HD) < HD // 2, -1.0, 1.0).astype(np.float32)[:, None]
    rope = np.stack([np.repeat(np.cos(angle), NH, axis=0), np.repeat(np.sin(angle) * sign, NH, axis=0)], axis=1)

    b1_chunks = np.asarray(L0_ffn_b1).reshape(NE, NC, P).transpose(0, 2, 1)
    w1_biases = np.concatenate([np.asarray(L0_ffn_w1), b1_chunks], axis=2)
    w2_bias = np.concatenate([np.asarray(L0_ffn_w2), np.asarray(L0_ffn_b2)[:, None]], axis=1)

    arrays = {
        "x_dram": x, "ctx_dram": ctx_1024, "w_self_dram": w_self, "w_cross_dram": w_cross,
        "b_proj_dram": np.asarray(L0_xattn_b_proj), "rope_dram": rope.astype(np.float32), "gate_dram": L0_ffn_gate_w,
        "w1_dram": w1_biases, "w2_dram": w2_bias,
    }
    arrays = {k: np.ascontiguousarray(v) for k, v in arrays.items()}
    nc = bacc.Bacc("TRN2", target_bir_lowering=False, num_devices=1)
    args = [nc.dram_tensor(k, v.shape, mybir.dt.from_np(v.dtype), kind="ExternalInput").ap() for k, v in arrays.items()]
    out = nc.dram_tensor("out_dram", (NB, S, D), F32, kind="ExternalOutput").ap()
    build(nc, *args, out)
    r = run(nc, [arrays], core_ids=[0])
    return r.results[0]["out_dram"]
```
